# Optimizing a Trainium2 kernel written in Bass

```python
import numpy as np
import jax
import jax.numpy as jnp

def _softmax(x, axis=-1):
    return jax.nn.softmax(x, axis=axis)

def _gelu(x):
    return jax.nn.gelu(x, approximate=True)

def _silu(x):
    return jax.nn.silu(x)

def _sigmoid(x):
    return jax.nn.sigmoid(x)

def _layernorm(x, axis=-1, eps=1e-05):
    m = jnp.mean(x, axis=axis, keepdims=True)
    v = jnp.var(x, axis=axis, keepdims=True)
    return (x - m) / jnp.sqrt(v + eps)

def _scatter_add(tgt, idx, src, axis=0):
    return tgt.at[idx].add(src)

def _segment_sum(src, seg, n):
    return jax.ops.segment_sum(src, seg, n)
kernel_name = 'mk_prb_d2_jaxref_r4_56c8f0'

def setup_inputs(seed: int=0):
    np.random.seed(seed)
    _w = jnp.asarray

    def _L0_attn_setup():
        import jax, jax.numpy as jnp
        import numpy as np
        B, N, D = (4, 1024, 256)
        H, F = (16, 64)
        HD = D // H
        EPS_ATTN = 1e-08
        EPS_LN = 1e-05

        def _layernorm(x, gamma, beta):
            mu = jnp.mean(x, axis=-1, keepdims=True)
            var = jnp.var(x, axis=-1, keepdims=True)
            return (x - mu) * jax.lax.rsqrt(var + EPS_LN) * gamma + beta
        key = jax.random.key(seed)
        ks = jax.random.split(key, 10)

        def kaiming(k, shape):
            fan_in = shape[1]
            return jax.random.normal(k, shape, jnp.float32) * jnp.sqrt(2.0 / fan_in)
        pm = jax.random.normal(ks[0], (H, HD, F), jnp.float32)
        return {'x': jax.random.normal(ks[1], (B, N, D), jnp.float32), 'proj': pm, 'w_qkv': kaiming(ks[2], (3 * D, D)), 'w_out': kaiming(ks[3], (D, D)), 'b_out': jnp.zeros((D,), jnp.float32), 'gamma': jnp.ones((D,), jnp.float32), 'beta': jnp.zeros((D,), jnp.float32), 'w1': kaiming(ks[4], (4 * D, D)), 'b1': jnp.zeros((4 * D,), jnp.float32), 'w2': kaiming(ks[5], (D, 4 * D)), 'b2': jnp.zeros((D,), jnp.float32)}
    _L0_attn_in = _L0_attn_setup()

    def _L0_ffn_setup():
        import jax, jax.numpy as jnp
        import numpy as np
        TOP_K = 2
        key = jax.random.key(seed)
        ks = jax.random.split(key, 5)
        B, S, H, E = (2, 256, 256, 8)
        return {'hidden_states': jax.random.normal(ks[0], (B, S, H), dtype=jnp.float32), 'router_w': jax.random.normal(ks[1], (E, H), dtype=jnp.float32) * 0.02, 'router_b': jax.random.normal(ks[2], (E,), dtype=jnp.float32) * 0.02, 'expert_w': jax.random.normal(ks[3], (E, H, H), dtype=jnp.float32) * 0.02, 'expert_b': jax.random.normal(ks[4], (E, H), dtype=jnp.float32) * 0.02}
    _L0_ffn_in = _L0_ffn_setup()

    def _L1_attn_setup():
        import jax, jax.numpy as jnp
        import numpy as np
        import math
        B, S, E = (2, 512, 256)
        H, DC, DR = (16, 64, 128)
        HD = E // H

        def _linear_params(key, din, dout):
            k1, k2 = jax.random.split(key)
            bound = 1.0 / math.sqrt(din)
            w = jax.random.uniform(k1, (din, dout), minval=-bound, maxval=bound, dtype=jnp.float32)
            b = jax.random.uniform(k2, (dout,), minval=-bound, maxval=bound, dtype=jnp.float32)
            return (w, b)

        def _gelu(x):
            return jax.nn.gelu(x, approximate=False)

        def _rope_cos_sin(seq_len, d_rope):
            inv_freq = 1.0 / 10000.0 ** (jnp.arange(0, d_rope, 2, dtype=jnp.float32) / d_rope)
            t = jnp.arange(seq_len, dtype=jnp.float32)
            freqs = t[:, None] * inv_freq[None, :]
            emb = jnp.concatenate([freqs, freqs], axis=-1)
            return (jnp.cos(emb), jnp.sin(emb))

        def _apply_rope(x, cos, sin):
            d = x.shape[-1]
            x1, x2 = (x[..., :d // 2], x[..., d // 2:])
            rot = jnp.concatenate([-x2, x1], axis=-1)
            return x * cos + rot * sin
        key = jax.random.key(seed)
        ks = jax.random.split(key, 10)
        x = jax.random.normal(ks[0], (B, S, E), dtype=jnp.float32)
        wq, bq = _linear_params(ks[1], E, DC)
        wqc, bqc = _linear_params(ks[2], DC, E - DR)
        wqr, bqr = _linear_params(ks[3], E, DR)
        wkv, bkv = _linear_params(ks[4], E, DC)
        wkr, bkr = _linear_params(ks[5], E, DR)
        wkc, bkc = _linear_params(ks[6], DC, E - DR)
        wv, bv = _linear_params(ks[7], DC, E)
        wo, bo = _linear_params(ks[8], E, E)
        return dict(x=x, wq=wq, bq=bq, wqc=wqc, bqc=bqc, wqr=wqr, bqr=bqr, wkv=wkv, bkv=bkv, wkr=wkr, bkr=bkr, wkc=wkc, bkc=bkc, wv=wv, bv=bv, wo=wo, bo=bo)
    _L1_attn_in = _L1_attn_setup()

    def _L1_ffn_setup():
        import jax, jax.numpy as jnp
        import numpy as np
        DIM = 256
        DEPTH = 2
        HEADS = 8
        DIM_HEAD = 64
        WINDOW = 128
        INNER = HEADS * DIM_HEAD
        HID = int(DIM * 4 * 2 / 3)
        B, N = (2, 2048)
        QK_SCALE = 8.0

        def shift_token(t):
            t1, t2 = jnp.split(t, 2, axis=-1)
            t2 = jnp.pad(t2, ((0, 0), (1, 0), (0, 0)))[:, :-1]
            return jnp.concatenate([t1, t2], axis=-1)

        def l2norm(t):
            return t / jnp.clip(jnp.linalg.norm(t, axis=-1, keepdims=True), 1e-12)

        def rotate_half(x):
            x1, x2 = jnp.split(x, 2, axis=-1)
            return jnp.concatenate([-x2, x1], axis=-1)

        def rotary_xpos(q, k):
            n = q.shape[-2]
            half_idx = jnp.arange(0, DIM_HEAD, 2, dtype=jnp.float32)
            inv_freq = 1.0 / 10000.0 ** (half_idx / DIM_HEAD)
            t = jnp.arange(n, dtype=jnp.float32)
            freqs = t[:, None] * inv_freq[None, :]
            freqs = jnp.concatenate([freqs, freqs], axis=-1)
            base = (half_idx + 0.4 * DIM_HEAD) / (1.4 * DIM_HEAD)
            power = (t - n // 2) / float(WINDOW // 2)
            scale = base[None, :] ** power[:, None]
            scale = jnp.concatenate([scale, scale], axis=-1)
            cos, sin = (jnp.cos(freqs), jnp.sin(freqs))
            q = q * cos * scale + rotate_half(q) * sin * scale
            k = k * cos / scale + rotate_half(k) * sin / scale
            return (q, k)

        def local_attention(q, k, v):
            b, h, n, d = q.shape
            w = n // WINDOW
            bq = q.reshape(b, h, w, WINDOW, d) * QK_SCALE
            bk = k.reshape(b, h, w, WINDOW, d)
            bv = v.reshape(b, h, w, WINDOW, d)

            def look_around(t):
                p = jnp.pad(t, ((0, 0), (0, 0), (1, 0), (0, 0), (0, 0)))
                return jnp.concatenate([p[:, :, :w], p[:, :, 1:]], axis=3)
            bk, bv = (look_around(bk), look_around(bv))
            bt = jnp.arange(n).reshape(w, WINDOW)
            btp = jnp.pad(bt, ((1, 0), (0, 0)), constant_values=-1)
            btk = jnp.concatenate([btp[:w], btp[1:]], axis=1)
            sim = jnp.einsum('bhwid,bhwjd->bhwij', bq, bk)
            i = bt[:, :, None]
            j = btk[:, None, :]
            mask = (i < j) | (i > j + WINDOW) | (j == -1)
            sim = jnp.where(mask, -jnp.finfo(sim.dtype).max, sim)
            attn = jax.nn.softmax(sim, axis=-1)
            out = jnp.einsum('bhwij,bhwjd->bhwid', attn, bv)
            return out.reshape(b, h, n, d)

        def _layer(x, wqkv, qs, ksc, wo, lg, lb, w1, b1, w2, b2):
            b, n, _ = x.shape
            h = shift_token(x)
            qkv = h @ wqkv
            q, k, v = jnp.split(qkv, 3, axis=-1)
            to_heads = lambda t: t.reshape(b, n, HEADS, DIM_HEAD).transpose(0, 2, 1, 3)
            q, k, v = (to_heads(q), to_heads(k), to_heads(v))
            q = l2norm(q) * qs
            k = l2norm(k) * ksc
            q, k = rotary_xpos(q, k)
            o = local_attention(q, k, v)
            o = o.transpose(0, 2, 1, 3).reshape(b, n, INNER)
            x = x + o @ wo
            h = shift_token(x)
            mu = h.mean(-1, keepdims=True)
            var = h.var(-1, keepdims=True)
            h = (h - mu) / jnp.sqrt(var + 1e-05) * lg + lb
            h = h @ w1 + b1
            a, g = jnp.split(h, 2, axis=-1)
            h = a * jax.nn.gelu(g, approximate=False)
            x = x + h @ w2 + b2
            return x
        key = jax.random.key(seed)
        ks = jax.random.split(key, 6)
        return {'x': jax.random.normal(ks[0], (B, N, DIM), jnp.float32), 'wqkv': jax.random.normal(ks[1], (DEPTH, DIM, 3 * INNER), jnp.float32) * 0.02, 'q_scale': jnp.ones((DEPTH, DIM_HEAD), jnp.float32), 'k_scale': jnp.ones((DEPTH, DIM_HEAD), jnp.float32), 'wo': jax.random.normal(ks[2], (DEPTH, INNER, DIM), jnp.float32) * 0.02, 'ln_g': jnp.ones((DEPTH, DIM), jnp.float32), 'ln_b': jnp.zeros((DEPTH, DIM), jnp.float32), 'w1': jax.random.normal(ks[3], (DEPTH, DIM, 2 * HID), jnp.float32) * 0.02, 'b1': jnp.zeros((DEPTH, 2 * HID), jnp.float32), 'w2': jax.random.normal(ks[4], (DEPTH, HID, DIM), jnp.float32) * 0.02, 'b2': jnp.zeros((DEPTH, DIM), jnp.float32)}
    _L1_ffn_in = _L1_ffn_setup()
    _d = {'L0_attn_x': _L0_attn_in['x'], 'L0_attn_proj': _L0_attn_in['proj'], 'L0_attn_w_qkv': _L0_attn_in['w_qkv'], 'L0_attn_w_out': _L0_attn_in['w_out'], 'L0_attn_b_out': _L0_attn_in['b_out'], 'L0_attn_gamma': _L0_attn_in['gamma'], 'L0_attn_beta': _L0_attn_in['beta'], 'L0_attn_w1': _L0_attn_in['w1'], 'L0_attn_b1': _L0_attn_in['b1'], 'L0_attn_w2': _L0_attn_in['w2'], 'L0_attn_b2': _L0_attn_in['b2'], 'L0_ffn_router_w': _L0_ffn_in['router_w'], 'L0_ffn_router_b': _L0_ffn_in['router_b'], 'L0_ffn_expert_w': _L0_ffn_in['expert_w'], 'L0_ffn_expert_b': _L0_ffn_in['expert_b'], 'L1_attn_wq': _L1_attn_in['wq'], 'L1_attn_bq': _L1_attn_in['bq'], 'L1_attn_wqc': _L1_attn_in['wqc'], 'L1_attn_bqc': _L1_attn_in['bqc'], 'L1_attn_wqr': _L1_attn_in['wqr'], 'L1_attn_bqr': _L1_attn_in['bqr'], 'L1_attn_wkv': _L1_attn_in['wkv'], 'L1_attn_bkv': _L1_attn_in['bkv'], 'L1_attn_wkr': _L1_attn_in['wkr'], 'L1_attn_bkr': _L1_attn_in['bkr'], 'L1_attn_wkc': _L1_attn_in['wkc'], 'L1_attn_bkc': _L1_attn_in['bkc'], 'L1_attn_wv': _L1_attn_in['wv'], 'L1_attn_bv': _L1_attn_in['bv'], 'L1_attn_wo': _L1_attn_in['wo'], 'L1_attn_bo': _L1_attn_in['bo'], 'L1_ffn_wqkv': _L1_ffn_in['wqkv'], 'L1_ffn_q_scale': _L1_ffn_in['q_scale'], 'L1_ffn_k_scale': _L1_ffn_in['k_scale'], 'L1_ffn_wo': _L1_ffn_in['wo'], 'L1_ffn_ln_g': _L1_ffn_in['ln_g'], 'L1_ffn_ln_b': _L1_ffn_in['ln_b'], 'L1_ffn_w1': _L1_ffn_in['w1'], 'L1_ffn_b1': _L1_ffn_in['b1'], 'L1_ffn_w2': _L1_ffn_in['w2'], 'L1_ffn_b2': _L1_ffn_in['b2']}
    _x0 = _d['L0_attn_x']
    _d['L0_attn_x'] = jax.random.normal(jax.random.fold_in(jax.random.key(seed), 1), (1, 4096, 256), dtype=_x0.dtype)
    del _x0
    return _d

def reference(L0_attn_x, L0_attn_proj, L0_attn_w_qkv, L0_attn_w_out, L0_attn_b_out, L0_attn_gamma, L0_attn_beta, L0_attn_w1, L0_attn_b1, L0_attn_w2, L0_attn_b2, L0_ffn_router_w, L0_ffn_router_b, L0_ffn_expert_w, L0_ffn_expert_b, L1_attn_wq, L1_attn_bq, L1_attn_wqc, L1_attn_bqc, L1_attn_wqr, L1_attn_bqr, L1_attn_wkv, L1_attn_bkv, L1_attn_wkr, L1_attn_bkr, L1_attn_wkc, L1_attn_bkc, L1_attn_wv, L1_attn_bv, L1_attn_wo, L1_attn_bo, L1_ffn_wqkv, L1_ffn_q_scale, L1_ffn_k_scale, L1_ffn_wo, L1_ffn_ln_g, L1_ffn_ln_b, L1_ffn_w1, L1_ffn_b1, L1_ffn_w2, L1_ffn_b2):

    def _L0_attn_ref(x, proj, w_qkv, w_out, b_out, gamma, beta, w1, b1, w2, b2):
        import jax, jax.numpy as jnp
        import numpy as np
        B, N, D = (4, 1024, 256)
        H, F = (16, 64)
        HD = D // H
        EPS_ATTN = 1e-08
        EPS_LN = 1e-05

        def _layernorm(x, gamma, beta):
            mu = jnp.mean(x, axis=-1, keepdims=True)
            var = jnp.var(x, axis=-1, keepdims=True)
            return (x - mu) * jax.lax.rsqrt(var + EPS_LN) * gamma + beta
        residual = x
        b, n, d = x.shape
        qkv = x @ w_qkv.T
        q, k, v = jnp.split(qkv, 3, axis=-1)

        def to_heads(t):
            return t.reshape(b, n, H, HD).transpose(0, 2, 1, 3)
        q, k, v = (to_heads(q), to_heads(k), to_heads(v))
        q_f = jax.nn.elu(jnp.einsum('bhnd,hdf->bhnf', q, proj)) + 1.0
        k_f = jax.nn.elu(jnp.einsum('bhnd,hdf->bhnf', k, proj)) + 1.0
        kv = jnp.einsum('bhnf,bhnd->bhfd', k_f, v)
        attn = jnp.einsum('bhnf,bhfd->bhnd', q_f, kv)
        k_sum = jnp.sum(k_f, axis=2)
        z = 1.0 / (jnp.einsum('bhnf,bhf->bhn', q_f, k_sum) + EPS_ATTN)
        attn = attn * z[..., None]
        attn = attn.transpose(0, 2, 1, 3).reshape(b, n, d)
        x = residual + attn @ w_out.T + b_out
        x = _layernorm(x, gamma, beta)
        h = jax.nn.gelu(x @ w1.T + b1, approximate=False)
        x = x + h @ w2.T + b2
        x = _layernorm(x, gamma, beta)
        return x

    def _L0_ffn_ref(hidden_states, router_w, router_b, expert_w, expert_b):
        import jax, jax.numpy as jnp
        import numpy as np
        TOP_K = 2
        logits = jnp.einsum('bsh,eh->bse', hidden_states, router_w) + router_b
        routing_weights = jax.nn.softmax(logits, axis=-1)
        _, top_k_indices = jax.lax.top_k(routing_weights, TOP_K)
        E = router_w.shape[0]
        mask = jax.nn.one_hot(top_k_indices, E, dtype=hidden_states.dtype).sum(axis=-2)
        out = jnp.einsum('bse,ehd,bsd->bsh', mask, expert_w, hidden_states)
        out = out + jnp.einsum('bse,eh->bsh', mask, expert_b)
        return out

    def _L1_attn_ref(x, wq, bq, wqc, bqc, wqr, bqr, wkv, bkv, wkr, bkr, wkc, bkc, wv, bv, wo, bo):
        import jax, jax.numpy as jnp
        import numpy as np
        import math
        B, S, E = (2, 512, 256)
        H, DC, DR = (16, 64, 128)
        HD = E // H

        def _linear_params(key, din, dout):
            k1, k2 = jax.random.split(key)
            bound = 1.0 / math.sqrt(din)
            w = jax.random.uniform(k1, (din, dout), minval=-bound, maxval=bound, dtype=jnp.float32)
            b = jax.random.uniform(k2, (dout,), minval=-bound, maxval=bound, dtype=jnp.float32)
            return (w, b)

        def _gelu(x):
            return jax.nn.gelu(x, approximate=False)

        def _rope_cos_sin(seq_len, d_rope):
            inv_freq = 1.0 / 10000.0 ** (jnp.arange(0, d_rope, 2, dtype=jnp.float32) / d_rope)
            t = jnp.arange(seq_len, dtype=jnp.float32)
            freqs = t[:, None] * inv_freq[None, :]
            emb = jnp.concatenate([freqs, freqs], axis=-1)
            return (jnp.cos(emb), jnp.sin(emb))

        def _apply_rope(x, cos, sin):
            d = x.shape[-1]
            x1, x2 = (x[..., :d // 2], x[..., d // 2:])
            rot = jnp.concatenate([-x2, x1], axis=-1)
            return x * cos + rot * sin
        b, s, _ = x.shape
        cq = _gelu(x @ wq + bq)
        q_c = cq @ wqc + bqc
        q_r = x @ wqr + bqr
        ckv = _gelu(x @ wkv + bkv)
        k_r = x @ wkr + bkr
        k_c = ckv @ wkc + bkc
        v = (ckv @ wv + bv).reshape(b, s, H, HD).transpose(0, 2, 1, 3)
        cos, sin = _rope_cos_sin(s, DR)
        q_r = _apply_rope(q_r, cos, sin)
        k_r = _apply_rope(k_r, cos, sin)
        q = _gelu(jnp.concatenate([q_c, q_r], axis=-1)).reshape(b, s, H, HD).transpose(0, 2, 1, 3)
        k = _gelu(jnp.concatenate([k_c, k_r], axis=-1)).reshape(b, s, H, HD).transpose(0, 2, 1, 3)
        scale = 1.0 / math.sqrt(HD)
        scores = jnp.einsum('bhqd,bhkd->bhqk', q, k) * scale
        causal = jnp.triu(jnp.ones((s, s), dtype=bool), k=1)
        scores = jnp.where(causal[None, None], -jnp.inf, scores)
        attn = jax.nn.softmax(scores, axis=-1)
        out = jnp.einsum('bhqk,bhkd->bhqd', attn, v)
        out = out.transpose(0, 2, 1, 3).reshape(b, s, E)
        return out @ wo + bo

    def _L1_ffn_ref(x, wqkv, q_scale, k_scale, wo, ln_g, ln_b, w1, b1, w2, b2):
        import jax, jax.numpy as jnp
        import numpy as np
        DIM = 256
        DEPTH = 2
        HEADS = 8
        DIM_HEAD = 64
        WINDOW = 128
        INNER = HEADS * DIM_HEAD
        HID = int(DIM * 4 * 2 / 3)
        B, N = (2, 2048)
        QK_SCALE = 8.0

        def shift_token(t):
            t1, t2 = jnp.split(t, 2, axis=-1)
            t2 = jnp.pad(t2, ((0, 0), (1, 0), (0, 0)))[:, :-1]
            return jnp.concatenate([t1, t2], axis=-1)

        def l2norm(t):
            return t / jnp.clip(jnp.linalg.norm(t, axis=-1, keepdims=True), 1e-12)

        def rotate_half(x):
            x1, x2 = jnp.split(x, 2, axis=-1)
            return jnp.concatenate([-x2, x1], axis=-1)

        def rotary_xpos(q, k):
            n = q.shape[-2]
            half_idx = jnp.arange(0, DIM_HEAD, 2, dtype=jnp.float32)
            inv_freq = 1.0 / 10000.0 ** (half_idx / DIM_HEAD)
            t = jnp.arange(n, dtype=jnp.float32)
            freqs = t[:, None] * inv_freq[None, :]
            freqs = jnp.concatenate([freqs, freqs], axis=-1)
            base = (half_idx + 0.4 * DIM_HEAD) / (1.4 * DIM_HEAD)
            power = (t - n // 2) / float(WINDOW // 2)
            scale = base[None, :] ** power[:, None]
            scale = jnp.concatenate([scale, scale], axis=-1)
            cos, sin = (jnp.cos(freqs), jnp.sin(freqs))
            q = q * cos * scale + rotate_half(q) * sin * scale
            k = k * cos / scale + rotate_half(k) * sin / scale
            return (q, k)

        def local_attention(q, k, v):
            b, h, n, d = q.shape
            w = n // WINDOW
            bq = q.reshape(b, h, w, WINDOW, d) * QK_SCALE
            bk = k.reshape(b, h, w, WINDOW, d)
            bv = v.reshape(b, h, w, WINDOW, d)

            def look_around(t):
                p = jnp.pad(t, ((0, 0), (0, 0), (1, 0), (0, 0), (0, 0)))
                return jnp.concatenate([p[:, :, :w], p[:, :, 1:]], axis=3)
            bk, bv = (look_around(bk), look_around(bv))
            bt = jnp.arange(n).reshape(w, WINDOW)
            btp = jnp.pad(bt, ((1, 0), (0, 0)), constant_values=-1)
            btk = jnp.concatenate([btp[:w], btp[1:]], axis=1)
            sim = jnp.einsum('bhwid,bhwjd->bhwij', bq, bk)
            i = bt[:, :, None]
            j = btk[:, None, :]
            mask = (i < j) | (i > j + WINDOW) | (j == -1)
            sim = jnp.where(mask, -jnp.finfo(sim.dtype).max, sim)
            attn = jax.nn.softmax(sim, axis=-1)
            out = jnp.einsum('bhwij,bhwjd->bhwid', attn, bv)
            return out.reshape(b, h, n, d)

        def _layer(x, wqkv, qs, ksc, wo, lg, lb, w1, b1, w2, b2):
            b, n, _ = x.shape
            h = shift_token(x)
            qkv = h @ wqkv
            q, k, v = jnp.split(qkv, 3, axis=-1)
            to_heads = lambda t: t.reshape(b, n, HEADS, DIM_HEAD).transpose(0, 2, 1, 3)
            q, k, v = (to_heads(q), to_heads(k), to_heads(v))
            q = l2norm(q) * qs
            k = l2norm(k) * ksc
            q, k = rotary_xpos(q, k)
            o = local_attention(q, k, v)
            o = o.transpose(0, 2, 1, 3).reshape(b, n, INNER)
            x = x + o @ wo
            h = shift_token(x)
            mu = h.mean(-1, keepdims=True)
            var = h.var(-1, keepdims=True)
            h = (h - mu) / jnp.sqrt(var + 1e-05) * lg + lb
            h = h @ w1 + b1
            a, g = jnp.split(h, 2, axis=-1)
            h = a * jax.nn.gelu(g, approximate=False)
            x = x + h @ w2 + b2
            return x
        for l in range(DEPTH):
            x = _layer(x, wqkv[l], q_scale[l], k_scale[l], wo[l], ln_g[l], ln_b[l], w1[l], b1[l], w2[l], b2[l])
        return x
    x = L0_attn_x
    xn = _layernorm(x, axis=-1)
    x = x + _L0_attn_ref(xn, L0_attn_proj, L0_attn_w_qkv, L0_attn_w_out, L0_attn_b_out, L0_attn_gamma, L0_attn_beta, L0_attn_w1, L0_attn_b1, L0_attn_w2, L0_attn_b2) + _L0_ffn_ref(xn, L0_ffn_router_w, L0_ffn_router_b, L0_ffn_expert_w, L0_ffn_expert_b)
    xn = _layernorm(x, axis=-1)
    x = x + _L1_attn_ref(xn, L1_attn_wq, L1_attn_bq, L1_attn_wqc, L1_attn_bqc, L1_attn_wqr, L1_attn_bqr, L1_attn_wkv, L1_attn_bkv, L1_attn_wkr, L1_attn_bkr, L1_attn_wkc, L1_attn_bkc, L1_attn_wv, L1_attn_bv, L1_attn_wo, L1_attn_bo) + _L1_ffn_ref(xn, L1_ffn_wqkv, L1_ffn_q_scale, L1_ffn_k_scale, L1_ffn_wo, L1_ffn_ln_g, L1_ffn_ln_b, L1_ffn_w1, L1_ffn_b1, L1_ffn_w2, L1_ffn_b2)
    return x

_drawn_inputs = setup_inputs


def setup_inputs(seed=0):
    import zlib

    import numpy as np

    out = dict(_drawn_inputs(seed))
    spreads = {'L0_attn_b_out': (0.0, 0.1),
     'L0_attn_gamma': (1.0, 0.2),
     'L0_attn_beta': (0.0, 0.1),
     'L0_attn_b1': (0.0, 0.1),
     'L0_attn_b2': (0.0, 0.1),
     'L1_ffn_q_scale': (1.0, 0.6),
     'L1_ffn_k_scale': (1.0, 0.6),
     'L1_ffn_ln_g': (1.0, 0.6),
     'L1_ffn_ln_b': (0.0, 0.8),
     'L1_ffn_b1': (0.0, 0.8),
     'L1_ffn_b2': (0.0, 0.269)}
    factors = {'L0_attn_proj': 3.334,
     'L0_ffn_expert_b': 3.794,
     'L1_attn_wq': 8.0,
     'L1_attn_bq': 8.0,
     'L1_attn_wqc': 8.0,
     'L1_attn_bqc': 8.0,
     'L1_attn_wqr': 8.0,
     'L1_attn_bqr': 8.0,
     'L1_attn_wkv': 7.153,
     'L1_attn_bkv': 8.0,
     'L1_attn_wkr': 8.0,
     'L1_attn_bkr': 8.0,
     'L1_attn_wkc': 8.0,
     'L1_attn_bkc': 8.0,
     'L1_attn_wv': 3.327,
     'L1_attn_bv': 10.571,
     'L1_attn_bo': 12.531,
     'L1_ffn_wqkv': 2.762,
     'L1_ffn_wo': 2.69,
     'L1_ffn_w1': 3.353,
     'L1_ffn_w2': 3.316}
    for name, (base, spread) in spreads.items():
        noise = np.random.default_rng([zlib.crc32(name.encode()), seed]).standard_normal(out[name].shape)
        drawn = base * np.exp(spread * noise) if base else spread * noise
        out[name] = jnp.asarray(drawn.astype(out[name].dtype))
    for name, factor in factors.items():
        out[name] = (out[name] * factor).astype(out[name].dtype)
    return out
```

```python
from contextlib import ExitStack

import concourse.bass as bass
from concourse import mybir

F32 = mybir.dt.float32
BF16 = mybir.dt.bfloat16
U32 = mybir.dt.uint32
ACT = mybir.ActivationFunctionType
ALU = mybir.AluOpType
AX = mybir.AxisListType

P = 128
N = 4096
D = 256
DC = D // P
SUB = 4
GROUP = SUB * P
NG = N // GROUP
NT = N // P
EPS = 1e-5

H0 = 16
HD0 = D // H0
F0 = 64
PAIRS = H0 // 2
VW = HD0 + 1
FF0 = 4 * D
E0 = 8


class Frame:

    def __init__(self, nc, name):
        self.nc = nc
        self.name = name
        self.ctx = ExitStack()
        self.sems = []
        self.blocks = ExitStack()

    def __enter__(self):
        self.ctx.__enter__()
        return self

    def __exit__(self, *a):
        self.blocks.close()
        if self.sems and a[0] is None:
            self.nc.clear_and_free_semaphores(self.sems)
            self.nc.all_engine_barrier()
        return self.ctx.__exit__(*a)

    def sb(self, name, shape, dt=F32):
        return self.ctx.enter_context(self.nc.sbuf_tensor(f"{self.name}_{name}", shape, dt))

    def psum(self, name, shape, dt=F32):
        return self.ctx.enter_context(self.nc.psum_tensor(f"{self.name}_{name}", shape, dt))

    def sem(self, name):
        self.sems.append(self.nc.alloc_semaphore(name=f"{self.name}_{name}"))
        return self.sems[-1]

    def block(self):
        return self.blocks.enter_context(self.nc.Block())


def rows(w):
    return w.rearrange("(c p) n -> p c n", p=P)


def spread(v):
    return v.rearrange("(a n) -> a n", a=1).partition_broadcast(P)


def tiles(t):
    return t.rearrange("(g s p) d -> g p s d", s=SUB, p=P)


def constants(nc, ident, identb, causal_q, causal_k):
    with Frame(nc, "const") as f:
        made = f.sem("const_made")
        block = f.block()

        @block.gpsimd
        def _(pool):
            nc.gpsimd.memset(ident[:, :], 0.0).then_inc(made, 1)
            nc.gpsimd.memset(identb[:, :], 0.0).then_inc(made, 1)
            nc.gpsimd.memset(causal_q[:, :], 0.0).then_inc(made, 1)
            nc.gpsimd.memset(causal_k[:, :], 0.0).then_inc(made, 1)
            pool.wait_ge(made, 4)
            for m in (ident, identb):
                nc.gpsimd.affine_select(out=m[:, :], in_=m[:, :], compare_op=ALU.not_equal, fill=1.0,
                                        base=0, pattern=[[-1, P]], channel_multiplier=1).then_inc(made, 1)
            nc.gpsimd.affine_select(out=causal_q[:, :], in_=causal_q[:, :], compare_op=ALU.is_ge, fill=-1e30,
                                    base=0, pattern=[[-1, P]], channel_multiplier=1).then_inc(made, 1)
            nc.gpsimd.affine_select(out=causal_k[:, :], in_=causal_k[:, :], compare_op=ALU.is_ge, fill=-1e30,
                                    base=0, pattern=[[1, P]], channel_multiplier=-1).then_inc(made, 1)
            pool.wait_ge(made, 8)


def linear_attention_keys(nc, x, w_qkvT, projbd, kvbd, ident, xn_d, xnT_d):
    with Frame(nc, "keys") as f:
        wkv = f.sb("wkv", [P, DC, 2 * D])
        xin = f.sb("xin", [P, 2, SUB, D])
        xn = f.sb("xn", [P, 2, SUB, D])
        stats = f.sb("stats", [P, 2, SUB, 6])
        mv = f.sb("mv", [P, 2, SUB, 2])
        ve = f.sb("ve", [P, 2, SUB])
        half = f.sb("half", [P, SUB])
        eps = f.sb("eps", [P, SUB])
        rstd = f.sb("rstd", [P, 2, SUB])
        xnT = f.sb("xnT", [P, 2, DC, GROUP])
        kT = f.sb("kT", [P, DC, GROUP])
        below = f.sb("below", [P, 2, 2, GROUP])
        ez = f.sb("ez", [P, 2, 2, GROUP])
        kf = f.sb("kf", [P, 2, 2, GROUP])
        v1 = f.sb("v1", [P, 2, H0, VW])
        zeros = f.sb("zeros", [P, PAIRS * 2 * VW])
        tr = f.psum("tr", [P, 2, 512])
        kp = f.psum("kp", [P, 1, 512])
        vp = f.psum("vp", [P, 2, 512])
        fp = f.psum("fp", [P, 2, 512])
        kv = f.psum("kv", [P, 512])

        weights = f.sem("weights")
        prepared = f.sem("prepared")
        loaded = [f.sem(f"x_loaded{u}") for u in range(2)]
        x_used = f.sem("x_used")
        stats_done = f.sem("stats_done")
        pace = f.sem("pace")
        var_done = f.sem("var_done")
        var_eps = f.sem("var_eps")
        rstd_done = f.sem("rstd_done")
        xn_done = f.sem("xn_done")
        tr_done = f.sem("tr_done")
        xnT_done = f.sem("xnT_done")
        kp_done = f.sem("kp_done")
        kT_done = f.sem("kT_done")
        vp_done = f.sem("vp_done")
        v_done = f.sem("v_done")
        fp_done = f.sem("fp_done")
        below_done = f.sem("below_done")
        ez_done = f.sem("ez_done")
        kf_done = f.sem("kf_done")
        kv_done = f.sem("kv_done")
        stored = [f.sem(f"stored{u}") for u in range(2)]
        kv_out = f.sem("kv_out")
        kv_cleared = f.sem("kv_cleared")
        block = f.block()

        def features(s):
            return fp if s % 2 == 0 else tr

        xg, xng = tiles(x), tiles(xn_d)
        xnTg = xnT_d.rearrange("(c p) (g n) -> g p c n", p=P, n=GROUP)

        @block.sync
        def _(sp):
            sp.dma_start(wkv[:, :, :], rows(w_qkvT[:, D:3 * D])).then_inc(weights, 16)
            sp.dma_start(xin[:, 0, :, :], xg[0]).then_inc(loaded[0], 16)
            with sp.Fori(0, NG // 2) as i:
                for u in range(2):
                    g = 2 * i + u
                    sp.wait_ge(x_used, g + 1)
                    sp.dma_start(xin[:, 1 - u, :, :], xg[(g + 1) % NG]).then_inc(loaded[1 - u], 16)
                    sp.wait_ge(xn_done, 4 * g + 4)
                    sp.dma_start(xng[g], xn[:, u, :, :]).then_inc(stored[u], 16)
                    sp.wait_ge(xnT_done, 4 * g + 4)
                    sp.dma_start(xnTg[g], xnT[:, u, :, :]).then_inc(stored[u], 16)
            sp.wait_ge(loaded[0], 16 * (NG // 2 + 1))
            for u in range(2):
                sp.wait_ge(stored[u], 32 + 32 * (NG // 2))

        @block.gpsimd
        def _(pool):
            nc.gpsimd.memset(half[:, :], -0.5).then_inc(prepared, 1)
            nc.gpsimd.memset(eps[:, :], EPS).then_inc(prepared, 1)
            nc.gpsimd.memset(zeros[:, :], 0.0).then_inc(prepared, 1)
            nc.gpsimd.memset(v1[:, :, :, :], 1.0).then_inc(prepared, 1)
            pool.wait_ge(prepared, 4)
            with pool.Fori(0, NG // 2) as i:
                for u in range(2):
                    g = 2 * i + u
                    pool.wait_ge(var_done, 4 * g + 4)
                    nc.gpsimd.tensor_tensor(ve[:, u, :], mv[:, u, :, 1], eps[:, :], ALU.add).then_inc(var_eps, 1)
                    pool.wait_ge(var_eps, g + 1)
                    nc.gpsimd.tensor_tensor(rstd[:, u, :], ve[:, u, :], half[:, :], ALU.pow).then_inc(rstd_done, 1)

        @block.vector
        def _(dve):
            dve.sem_inc(x_used, 1)
            nc.vector.memset(kvbd[:, :, :], 0.0).then_inc(kv_cleared, 1)
            with dve.Fori(0, NG // 2) as i:
                for u in range(2):
                    g = 2 * i + u
                    dve.wait_ge(loaded[u], 16 * i + 16)
                    for s in range(SUB):
                        nc.vector.bn_stats(stats[:, u, s, :], xin[:, u, s, :]).then_inc(stats_done, 1)
                    dve.wait_ge(stats_done, 4 * g + 4)
                    dve.sem_inc(pace, 1)
                    for s in range(SUB):
                        nc.vector.bn_aggr(mv[:, u, s, :], stats[:, u, s, :]).then_inc(var_done, 1)
                    dve.wait_ge(var_done, 4 * g + 4)
                    dve.wait_ge(rstd_done, g + 1)
                    dve.wait_ge(stored[u], 32 * i + 32)
                    for s in range(SUB):
                        last = nc.vector.tensor_scalar(xn[:, u, s, :], xin[:, u, s, :], mv[:, u, s, 0:1],
                                                       rstd[:, u, s:s + 1], ALU.subtract, ALU.mult)
                        last.then_inc(xn_done, 1)
                    dve.wait_ge(xn_done, 4 * g + 4)
                    dve.sem_inc(x_used, 1)
                    if u == 0:
                        dve.wait_ge(prepared, 4)
                    for s in range(SUB):
                        dve.wait_ge(vp_done, 4 * g + s + 1)
                        dve.wait_ge(kv_done, 4 * g + s + 1)
                        nc.vector.tensor_copy(v1[:, s % 2, :, 0:HD0],
                                              vp[:, s % 2, 0:D].rearrange("p (h d) -> p h d", d=HD0)).then_inc(v_done, 1)
                        for c in range(2):
                            dve.wait_ge(ez_done, 2 * (4 * g + s) + c + 1)
                            nc.vector.scalar_tensor_tensor(kf[:, s % 2, c, :], features(s)[:, c, :], 0.0, ez[:, s % 2, c, :],
                                                           ALU.max, ALU.add).then_inc(kf_done, 1)
            dve.wait_ge(kv_done, NT + 2)
            dve.wait_ge(kv_cleared, 1)
            kvv = kv[:, 0:PAIRS * 2 * VW].rearrange("p (c j w) -> p c j w", c=PAIRS, j=2)
            kvo = kvbd[:, :, :].rearrange("p c (j w) -> p c j w", j=2)
            nc.vector.tensor_copy(kvo[0:F0, :, 0, :], kvv[0:F0, :, 0, :]).then_inc(kv_out, 1)
            nc.vector.tensor_copy(kvo[F0:P, :, 1, :], kvv[F0:P, :, 1, :]).then_inc(kv_out, 1)
            dve.wait_ge(kv_out, 2)

        @block.scalar
        def _(act):
            for u in range(2):
                act.sem_inc(stored[u], 32)
            with act.Fori(0, NG // 2) as i:
                for u in range(2):
                    g = 2 * i + u
                    act.wait_ge(stored[u], 32 * i + 32)
                    for s in range(SUB):
                        act.wait_ge(tr_done, 4 * g + s + 1)
                        nc.scalar.activation(xnT[:, u, :, P * s:P * s + P],
                                             tr[:, s % 2, 0:D].rearrange("p (c n) -> p c n", c=DC),
                                             ACT.Copy).then_inc(xnT_done, 1)
                    for m in range(DC):
                        act.wait_ge(kp_done, 2 * g + m + 1)
                        nc.scalar.activation(kT[:, m, :], kp[:, 0, :], ACT.Copy).then_inc(kT_done, 1)
                    for s in range(SUB):
                        t = 4 * g + s
                        for c in range(2):
                            act.wait_ge(fp_done, 2 * t + c + 1)
                            nc.scalar.activation(below[:, s % 2, c, :], features(s)[:, c, :], ACT.Relu, scale=-1.0).then_inc(below_done, 1)
                        for c in range(2):
                            act.wait_ge(below_done, 2 * t + c + 1)
                            nc.scalar.activation(ez[:, s % 2, c, :], below[:, s % 2, c, :], ACT.Exp, scale=-1.0).then_inc(ez_done, 1)

        @block.tensor
        def _(pe):
            pe.sem_inc(kv_done, 2)
            pe.wait_ge(weights, 16)
            pe.wait_ge(prepared, 4)
            nc.tensor.matmul(kv[:, 0:PAIRS * 2 * VW], ident[:, :], zeros[:, :], start=True, stop=True)

            def sums(g, s):
                pe.wait_ge(kf_done, 2 * (4 * g + s) + 2)
                pe.wait_ge(v_done, 4 * g + s + 1)
                for c in range(PAIRS):
                    last = nc.tensor.matmul(kv[:, 2 * VW * c:2 * VW * (c + 1)],
                                            kf[:, s % 2, c // 4, P * (c % 4):P * (c % 4) + P],
                                            v1[:, s % 2, 2 * c:2 * c + 2, :].rearrange("p h w -> p (h w)"),
                                            start=False, stop=True, skip_group_check=True)
                last.then_inc(kv_done, 1)

            with pe.Fori(0, NG // 2) as i:
                for u in range(2):
                    g = 2 * i + u
                    for s in range(SUB):
                        pe.wait_ge(xn_done, 4 * g + s + 1)
                        if s >= 2:
                            pe.wait_ge(xnT_done, 4 * g + s - 1)
                        for c in range(DC):
                            last = nc.tensor.transpose(tr[:, s % 2, P * c:P * c + P], xn[:, u, s, P * c:P * c + P], ident[:, :])
                        last.then_inc(tr_done, 1)
                    pe.wait_ge(xnT_done, 4 * g + 4)
                    for m in range(DC):
                        if m:
                            pe.wait_ge(kT_done, 2 * g + m)
                        for c in range(DC):
                            last = nc.tensor.matmul(kp[:, 0, :], wkv[:, c, P * m:P * m + P], xnT[:, u, c, :],
                                                    start=c == 0, stop=c == DC - 1)
                        last.then_inc(kp_done, 1)
                    for s in range(SUB):
                        for c in range(DC):
                            last = nc.tensor.matmul(vp[:, s % 2, 0:D], xnT[:, u, c, P * s:P * s + P], wkv[:, c, D:2 * D],
                                                    start=c == 0, stop=c == DC - 1)
                        last.then_inc(vp_done, 1)
                        pe.wait_ge(kT_done, 2 * g + 2)
                        for c in range(2):
                            if s >= 2:
                                pe.wait_ge(kf_done, 2 * (4 * g + s) - 3 + c)
                            nc.tensor.matmul(features(s)[:, c, :], kT[:, c, P * s:P * s + P],
                                             projbd[:, c, :], start=True, stop=True).then_inc(fp_done, 1)
                        if s:
                            sums(g, s - 1)
                    sums(g, SUB - 1)


def linear_attention_queries(nc, w_qkvT, w_outT, b_out, gamma, beta, projbd, kvbd, ident, xn_d, xnT_d, y_d):
    with Frame(nc, "queries") as f:
        wq = f.sb("wq", [P, DC, D])
        wo = f.sb("wo", [P, DC, D])
        bo = f.sb("bo", [P, D])
        gm = f.sb("gm", [P, D])
        bt = f.sb("bt", [P, D])
        half = f.sb("half", [P, SUB])
        eps = f.sb("eps", [P, SUB])
        xnT = f.sb("xnT", [P, 2, DC, GROUP])
        xn = f.sb("xn", [P, 2, SUB, D])
        xb = f.sb("xb", [P, SUB, D])
        qT = f.sb("qT", [P, DC, GROUP])
        below = f.sb("below", [P, 4, GROUP])
        ez = f.sb("ez", [P, 4, GROUP])
        qf = f.sb("qf", [P, PAIRS, GROUP])
        den = f.sb("den", [P, 2, H0])
        att = f.sb("att", [P, 2, D])
        attT = f.sb("attT", [P, 2, DC, P])
        r = f.sb("r", [P, SUB, D])
        stats = f.sb("stats", [P, SUB, 6])
        mv = f.sb("mv", [P, SUB, 2])
        ve = f.sb("ve", [P, SUB])
        rstd = f.sb("rstd", [P, SUB])
        yh = f.sb("yh", [P, SUB, D])
        y = f.sb("y", [P, SUB, D])
        qp = f.psum("qp", [P, 2, 512])
        ap = f.psum("ap", [P, 2, 512])
        tr = f.psum("tr", [P, 2, 512])
        op = f.psum("op", [P, 2, 512])

        weights = f.sem("weights")
        prepared = f.sem("prepared")
        loaded = [f.sem(f"loaded{u}") for u in range(2)]
        qp_done = f.sem("qp_done")
        qT_done = f.sem("qT_done")
        below_done = f.sem("below_done")
        ez_done = f.sem("ez_done")
        qf_done = f.sem("qf_done")
        ap_done = f.sem("ap_done")
        den_done = f.sem("den_done")
        rec_done = f.sem("rec_done")
        att_done = f.sem("att_done")
        tr_done = f.sem("tr_done")
        attT_done = f.sem("attT_done")
        op_done = f.sem("op_done")
        xb_done = f.sem("xb_done")
        r_done = f.sem("r_done")
        stats_done = f.sem("stats_done")
        pace = f.sem("pace")
        var_done = f.sem("var_done")
        var_eps = f.sem("var_eps")
        rstd_done = f.sem("rstd_done")
        yh_done = f.sem("yh_done")
        scaled = f.sem("scaled")
        y_done = f.sem("y_done")
        stored = f.sem("stored")
        block = f.block()

        def features(c):
            return qp[:, c % 4, :] if c % 4 < 2 else tr[:, c % 4 - 2, :]

        xng, yg = tiles(xn_d), tiles(y_d)
        xnTg = xnT_d.rearrange("(c p) (g n) -> g p c n", p=P, n=GROUP)

        @block.sync
        def _(sp):
            sp.dma_start(wq[:, :, :], rows(w_qkvT[:, 0:D])).then_inc(weights, 16)
            sp.dma_start(wo[:, :, :], rows(w_outT)).then_inc(weights, 16)
            sp.dma_start(bo[:, :], spread(b_out)).then_inc(weights, 16)
            sp.dma_start(gm[:, :], spread(gamma)).then_inc(weights, 16)
            sp.dma_start(bt[:, :], spread(beta)).then_inc(weights, 16)
            sp.dma_start(xnT[:, 0, :, :], xnTg[0]).then_inc(loaded[0], 16)
            sp.dma_start(xn[:, 0, :, :], xng[0]).then_inc(loaded[0], 16)
            with sp.Fori(0, NG // 2) as i:
                for u in range(2):
                    g = 2 * i + u
                    sp.wait_ge(qT_done, 2 * g + 2)
                    sp.wait_ge(xb_done, 4 * g + 4)
                    sp.dma_start(xnT[:, 1 - u, :, :], xnTg[(g + 1) % NG]).then_inc(loaded[1 - u], 16)
                    sp.dma_start(xn[:, 1 - u, :, :], xng[(g + 1) % NG]).then_inc(loaded[1 - u], 16)
                    sp.wait_ge(y_done, 4 * g + 8)
                    sp.dma_start(yg[g], y[:, :, :]).then_inc(stored, 16)
            sp.wait_ge(loaded[0], 32 * (NG // 2 + 1))
            sp.wait_ge(stored, 16 * NG + 16)

        @block.gpsimd
        def _(pool):
            pool.sem_inc(xb_done, 4)
            pool.sem_inc(stored, 16)
            nc.gpsimd.memset(half[:, :], -0.5).then_inc(prepared, 1)
            nc.gpsimd.memset(eps[:, :], EPS).then_inc(prepared, 1)
            pool.wait_ge(prepared, 2)
            pool.wait_ge(weights, 80)
            with pool.Fori(0, NG // 2) as i:
                for u in range(2):
                    g = 2 * i + u
                    pool.wait_ge(loaded[u], 32 * i + 32)
                    pool.wait_ge(r_done, 4 * g + 4)
                    for s in range(SUB):
                        nc.gpsimd.tensor_tensor(xb[:, s, :], xn[:, u, s, :], bo[:, :], ALU.add).then_inc(xb_done, 1)
                    pool.wait_ge(var_done, 4 * g + 4)
                    nc.gpsimd.tensor_tensor(ve[:, :], mv[:, :, 1], eps[:, :], ALU.add).then_inc(var_eps, 1)
                    pool.wait_ge(var_eps, g + 1)
                    nc.gpsimd.tensor_tensor(rstd[:, :], ve[:, :], half[:, :], ALU.pow).then_inc(rstd_done, 1)
                    pool.wait_ge(stored, 16 * g + 16)
                    for s in range(SUB):
                        pool.wait_ge(yh_done, 4 * g + s + 1)
                        nc.gpsimd.tensor_tensor(yh[:, s, :], yh[:, s, :], gm[:, :], ALU.mult).then_inc(scaled, 1)
                    for s in range(SUB):
                        pool.wait_ge(scaled, 4 * g + s + 1)
                        nc.gpsimd.tensor_tensor(y[:, s, :], yh[:, s, :], bt[:, :], ALU.add).then_inc(y_done, 1)

        @block.vector
        def _(dve):
            dve.sem_inc(r_done, 4)
            dve.sem_inc(y_done, 4)
            with dve.Fori(0, NG // 2) as i:
                for u in range(2):
                    g = 2 * i + u
                    for c in range(PAIRS):
                        dve.wait_ge(ez_done, 8 * g + c + 1)
                        nc.vector.scalar_tensor_tensor(qf[:, c, :], features(c), 0.0, ez[:, c % 4, :],
                                                       ALU.max, ALU.add).then_inc(qf_done, 1)
                    for s in range(SUB + 1):
                        if s < SUB:
                            t = 4 * g + s
                            a3 = ap[:, s % 2, 0:H0 * VW].rearrange("p (h w) -> p h w", w=VW)
                            dve.wait_ge(ap_done, t + 1)
                            nc.vector.tensor_scalar(den[:, s % 2, :], a3[:, :, HD0], 1e-8, None, ALU.add).then_inc(den_done, 1)
                            dve.wait_ge(den_done, t + 1)
                            nc.vector.reciprocal(den[:, s % 2, :], den[:, s % 2, :]).then_inc(rec_done, 1)
                            dve.wait_ge(rec_done, t + 1)
                            nc.vector.tensor_tensor(att[:, s % 2, :].rearrange("p (h w) -> p h w", w=HD0), a3[:, :, 0:HD0],
                                                    den[:, s % 2, :].unsqueeze(2).broadcast_to([P, H0, HD0]),
                                                    ALU.mult).then_inc(att_done, 1)
                        if s:
                            dve.wait_ge(op_done, 4 * g + s)
                            dve.wait_ge(xb_done, 4 * g + s + 4)
                            nc.vector.tensor_tensor(r[:, s - 1, :], op[:, (s - 1) % 2, 0:D], xb[:, s - 1, :], ALU.add).then_inc(r_done, 1)
                    for s in range(SUB):
                        dve.wait_ge(r_done, 4 * g + s + 5)
                        nc.vector.bn_stats(stats[:, s, :], r[:, s, :]).then_inc(stats_done, 1)
                    dve.wait_ge(stats_done, 4 * g + 4)
                    dve.sem_inc(pace, 1)
                    for s in range(SUB):
                        nc.vector.bn_aggr(mv[:, s, :], stats[:, s, :]).then_inc(var_done, 1)
                    dve.wait_ge(var_done, 4 * g + 4)
                    dve.wait_ge(rstd_done, g + 1)
                    dve.wait_ge(y_done, 4 * g + 4)
                    for s in range(SUB):
                        nc.vector.tensor_scalar(yh[:, s, :], r[:, s, :], mv[:, s, 0:1], rstd[:, s:s + 1],
                                                ALU.subtract, ALU.mult).then_inc(yh_done, 1)

        @block.scalar
        def _(act):
            act.sem_inc(qT_done, 2)
            with act.Fori(0, NG // 2) as i:
                for u in range(2):
                    g = 2 * i + u
                    for m in range(DC):
                        act.wait_ge(qp_done, 10 * g + m + 1)
                        nc.scalar.activation(qT[:, m, :], qp[:, m, :], ACT.Copy).then_inc(qT_done, 1)
                    for c in range(0, PAIRS, 2):
                        for b in range(2):
                            act.wait_ge(qp_done, 10 * g + DC + c + b + 1)
                            nc.scalar.activation(below[:, (c + b) % 4, :], features(c + b), ACT.Relu, scale=-1.0).then_inc(below_done, 1)
                        for b in range(2):
                            act.wait_ge(below_done, 8 * g + c + b + 1)
                            nc.scalar.activation(ez[:, (c + b) % 4, :], below[:, (c + b) % 4, :], ACT.Exp, scale=-1.0).then_inc(ez_done, 1)
                    for s in range(SUB):
                        act.wait_ge(tr_done, 4 * g + s + 1)
                        nc.scalar.activation(attT[:, s % 2, :, :], tr[:, s % 2, 0:D].rearrange("p (c n) -> p c n", c=DC),
                                             ACT.Copy).then_inc(attT_done, 1)

        @block.tensor
        def _(pe):
            pe.wait_ge(weights, 80)
            with pe.Fori(0, NG // 2) as i:
                for u in range(2):
                    g = 2 * i + u
                    pe.wait_ge(loaded[u], 32 * i + 32)
                    for m in range(DC):
                        for c in range(DC):
                            last = nc.tensor.matmul(qp[:, m, :], wq[:, c, P * m:P * m + P], xnT[:, u, c, :],
                                                    start=c == 0, stop=c == DC - 1)
                        last.then_inc(qp_done, 1)
                    for c in range(PAIRS):
                        if c < 2:
                            pe.wait_ge(qT_done, 2 * g + 4)
                        elif c >= 4:
                            pe.wait_ge(qf_done, 8 * g + c - 3)
                        nc.tensor.matmul(features(c), projbd[:, c // 4, P * (c % 4):P * (c % 4) + P],
                                         qT[:, c // 4, :], start=True, stop=True).then_inc(qp_done, 1)

                    def attend(s):
                        if s >= 2:
                            pe.wait_ge(att_done, 4 * g + s - 1)
                        for c in range(PAIRS):
                            last = nc.tensor.matmul(ap[:, s % 2, 2 * VW * c:2 * VW * (c + 1)], qf[:, c, P * s:P * s + P],
                                                    kvbd[:, c, :], start=True, stop=True, skip_group_check=True)
                        last.then_inc(ap_done, 1)

                    def turn(s):
                        pe.wait_ge(att_done, 4 * g + s + 1)
                        if s >= 2:
                            pe.wait_ge(attT_done, 4 * g + s - 1)
                        for c in range(DC):
                            last = nc.tensor.transpose(tr[:, s % 2, P * c:P * c + P], att[:, s % 2, P * c:P * c + P], ident[:, :])
                        last.then_inc(tr_done, 1)

                    def project(s):
                        pe.wait_ge(attT_done, 4 * g + s + 1)
                        if s >= 2:
                            pe.wait_ge(r_done, 4 * g + s + 3)
                        for c in range(DC):
                            last = nc.tensor.matmul(op[:, s % 2, 0:D], attT[:, s % 2, c, :], wo[:, c, :],
                                                    start=c == 0, stop=c == DC - 1)
                        last.then_inc(op_done, 1)

                    pe.wait_ge(qf_done, 8 * g + 8)
                    attend(0)
                    attend(1)
                    for s in range(SUB):
                        turn(s)
                        if s + 2 < SUB:
                            attend(s + 2)
                        project(s)


def experts(nc, x, router_wT, router_b, expert_wT, expert_b, ident, xnT_d, res_d):
    with Frame(nc, "moe") as f:
        wr = f.sb("wr", [P, DC, E0])
        br = f.sb("br", [P, E0])
        we = f.sb("we", [P, DC, E0, D])
        be = f.sb("be", [E0, D])
        order = f.sb("order", [P, SUB, E0])
        xnT = f.sb("xnT", [P, 2, DC, GROUP])
        xin = f.sb("xin", [P, 2, SUB, D])
        logit = f.sb("logit", [P, SUB, E0])
        best = f.sb("best", [P, SUB, E0])
        index = f.sb("index", [P, SUB, E0], U32)
        chosen = f.sb("chosen", [P, SUB, 2])
        first = f.sb("first", [P, SUB, E0])
        second = f.sb("second", [P, SUB, E0])
        mask = f.sb("mask", [P, SUB, E0])
        maskT = f.sb("maskT", [E0, SUB, P])
        acc = f.sb("acc", [P, 2, SUB, D])
        rp = f.psum("rp", [P, 512])
        mp = f.psum("mp", [P, 512])
        bp = f.psum("bp", [P, 2, 512])
        ep = f.psum("ep", [P, 4, 512])

        weights = f.sem("weights")
        order_made = f.sem("order_made")
        loaded = [f.sem(f"loaded{u}") for u in range(2)]
        rp_done = f.sem("rp_done")
        logit_done = f.sem("logit_done")
        pace = f.sem("pace")
        best_done = f.sem("best_done")
        index_done = f.sem("index_done")
        chosen_done = f.sem("chosen_done")
        each_done = f.sem("each_done")
        mask_done = f.sem("mask_done")
        mp_done = f.sem("mp_done")
        maskT_done = f.sem("maskT_done")
        bp_done = f.sem("bp_done")
        start_done = f.sem("start_done")
        ep_done = f.sem("ep_done")
        acc_done = f.sem("acc_done")
        stored = [f.sem(f"stored{u}") for u in range(2)]
        turn = f.sem("turn")
        block = f.block()
        xg, rg = tiles(x), tiles(res_d)
        xnTg = xnT_d.rearrange("(c p) (g n) -> g p c n", p=P, n=GROUP)

        @block.sync
        def _(sp):
            for u in range(2):
                sp.sem_inc(stored[u], 16)
            sp.dma_start(xnT[:, 0, :, :], xnTg[0]).then_inc(loaded[0], 16)
            sp.dma_start(xin[:, 0, :, :], xg[0]).then_inc(loaded[0], 16)
            sp.dma_start(wr[:, :, :], rows(router_wT)).then_inc(weights, 16)
            sp.dma_start(br[:, :], spread(router_b)).then_inc(weights, 16)
            sp.dma_start(we[:, :, :, :], expert_wT.rearrange("(c p) e h -> p c e h", p=P)).then_inc(weights, 16)
            sp.dma_start(be[:, :], expert_b).then_inc(weights, 16)
            with sp.Fori(0, NG // 2) as i:
                for u in range(2):
                    g = 2 * i + u
                    sp.wait_ge(acc_done, 32 * g + 32)
                    sp.sem_inc(turn, 1)
                    sp.dma_start(xnT[:, 1 - u, :, :], xnTg[(g + 1) % NG]).then_inc(loaded[1 - u], 16)
                    sp.dma_start(xin[:, 1 - u, :, :], xg[(g + 1) % NG]).then_inc(loaded[1 - u], 16)
                    sp.wait_ge(acc_done, 32 * g + 64)
                    sp.dma_start(rg[g], acc[:, u, :, :]).then_inc(stored[u], 16)
            sp.wait_ge(loaded[0], 32 * (NG // 2 + 1))
            for u in range(2):
                sp.wait_ge(stored[u], 16 + 16 * (NG // 2))

        @block.gpsimd
        def _(pool):
            nc.gpsimd.iota(order[:, :, :], pattern=[[0, SUB], [1, E0]], base=0, channel_multiplier=0,
                           allow_small_or_imprecise_dtypes=True).then_inc(order_made, 1)

        @block.vector
        def _(dve):
            dve.sem_inc(acc_done, 32)
            dve.wait_ge(order_made, 1)
            dve.wait_ge(weights, 64)
            with dve.Fori(0, NG // 2) as i:
                for u in range(2):
                    g = 2 * i + u
                    dve.wait_ge(rp_done, g + 1)
                    nc.vector.tensor_tensor(logit[:, :, :], rp[:, 0:SUB * E0].rearrange("p (s e) -> p s e", s=SUB),
                                            br[:, :].unsqueeze(1).broadcast_to([P, SUB, E0]), ALU.add).then_inc(logit_done, 1)
                    dve.wait_ge(logit_done, g + 1)
                    dve.sem_inc(pace, 1)
                    for s in range(SUB):
                        nc.vector.max(best[:, s, :], logit[:, s, :]).then_inc(best_done, 1)
                    dve.wait_ge(best_done, 4 * g + 4)
                    dve.sem_inc(pace, 1)
                    for s in range(SUB):
                        nc.vector.max_index(index[:, s, :], best[:, s, :], logit[:, s, :]).then_inc(index_done, 1)
                    dve.wait_ge(index_done, 4 * g + 4)
                    nc.vector.tensor_copy(chosen[:, :, :], index[:, :, 0:2]).then_inc(chosen_done, 1)
                    dve.wait_ge(chosen_done, g + 1)
                    for k, m in enumerate((first, second)):
                        nc.vector.tensor_tensor(m[:, :, :], order[:, :, :],
                                                chosen[:, :, k:k + 1].broadcast_to([P, SUB, E0]), ALU.is_equal).then_inc(each_done, 1)
                    dve.wait_ge(each_done, 2 * g + 2)
                    nc.vector.tensor_tensor(mask[:, :, :], first[:, :, :], second[:, :, :], ALU.add).then_inc(mask_done, 1)
                    dve.wait_ge(mask_done, g + 1)
                    dve.wait_ge(loaded[u], 32 * i + 32)
                    dve.wait_ge(stored[u], 16 * i + 16)
                    for s in range(SUB):
                        t = 4 * g + s
                        dve.wait_ge(bp_done, t + 1)
                        nc.vector.tensor_tensor(acc[:, u, s, :], bp[:, s % 2, 0:D], xin[:, u, s, :], ALU.add).then_inc(start_done, 1)
                        dve.wait_ge(start_done, t + 1)
                        for e in range(E0):
                            if e % 2 == 0:
                                dve.wait_ge(ep_done, 4 * t + e // 2 + 1)
                            if e:
                                dve.wait_ge(acc_done, 8 * t + e + 32)
                            nc.vector.scalar_tensor_tensor(acc[:, u, s, :], ep[:, e // 2, D * (e % 2):D * (e % 2) + D],
                                                           mask[:, s, e:e + 1], acc[:, u, s, :], ALU.mult, ALU.add).then_inc(acc_done, 1)

        @block.scalar
        def _(act):
            with act.Fori(0, NG) as g:
                act.wait_ge(mp_done, g + 1)
                nc.scalar.activation(maskT[:, :, :], mp[0:E0, 0:SUB * P].rearrange("p (s n) -> p s n", s=SUB),
                                     ACT.Copy).then_inc(maskT_done, 1)

        @block.tensor
        def _(pe):
            pe.wait_ge(weights, 64)
            with pe.Fori(0, NG // 2) as i:
                for u in range(2):
                    g = 2 * i + u
                    pe.wait_ge(loaded[u], 32 * i + 32)
                    for s in range(SUB):
                        for c in range(DC):
                            last = nc.tensor.matmul(rp[:, E0 * s:E0 * s + E0], xnT[:, u, c, P * s:P * s + P], wr[:, c, :],
                                                    start=c == 0, stop=c == DC - 1)
                    last.then_inc(rp_done, 1)
                    for s in range(SUB):
                        t = 4 * g + s
                        for b in range(4):
                            pe.wait_ge(acc_done, 8 * t + 2 * b + 26)
                            for c in range(DC):
                                last = nc.tensor.matmul(ep[:, b, :], xnT[:, u, c, P * s:P * s + P],
                                                        we[:, c, 2 * b:2 * b + 2, :].rearrange("p e h -> p (e h)"),
                                                        start=c == 0, stop=c == DC - 1)
                            last.then_inc(ep_done, 1)
                        if s == 0:
                            pe.wait_ge(mask_done, g + 1)
                            for k in range(SUB):
                                last = nc.tensor.transpose(mp[0:E0, P * k:P * k + P], mask[:, k, :], ident[:, :])
                            last.then_inc(mp_done, 1)
                            pe.wait_ge(maskT_done, g + 1)
                            for k in range(2):
                                nc.tensor.matmul(bp[:, k, 0:D], maskT[:, k, :], be[:, :], start=True, stop=True).then_inc(bp_done, 1)
                        elif s < 3:
                            pe.wait_ge(start_done, 4 * g + s)
                            nc.tensor.matmul(bp[:, (s + 1) % 2, 0:D], maskT[:, s + 1, :], be[:, :],
                                             start=True, stop=True).then_inc(bp_done, 1)


def feed_forward_0(nc, w1T, b1, w2T, b2, gamma, beta, ident, y_d, res_d, x1_d, xn1_d):
    FC = FF0 // P
    with Frame(nc, "ffn0") as f:
        w1 = f.sb("w1", [P, DC, FF0])
        w2 = f.sb("w2", [P, FC, D])
        b1c = f.sb("b1c", [P, FC])
        b2r = f.sb("b2r", [P, D])
        gm = f.sb("gm", [P, D])
        bt = f.sb("bt", [P, D])
        half = f.sb("half", [P, SUB])
        eps = f.sb("eps", [P, SUB])
        y = f.sb("y", [P, 2, SUB, D])
        res = f.sb("res", [P, 2, SUB, D])
        yT = f.sb("yT", [P, DC, GROUP])
        hT = f.sb("hT", [P, FC, GROUP])
        yb = f.sb("yb", [P, SUB, D])
        r = f.sb("r", [P, SUB, D])
        stats = f.sb("stats", [P, SUB, 6])
        mv = f.sb("mv", [P, SUB, 2])
        ve = f.sb("ve", [P, SUB])
        rstd = f.sb("rstd", [P, SUB])
        z = f.sb("z", [P, SUB, D])
        resb = f.sb("resb", [P, SUB, D])
        x1 = f.sb("x1", [P, SUB, D])
        xn1 = f.sb("xn1", [P, SUB, D])
        tr = f.psum("tr", [P, 2, 512])
        hp = f.psum("hp", [P, 4, 512])
        op = f.psum("op", [P, 2, 512])

        weights = f.sem("weights")
        prepared = f.sem("prepared")
        loaded = [f.sem(f"loaded{u}") for u in range(2)]
        tr_done = f.sem("tr_done")
        yT_done = f.sem("yT_done")
        hp_done = f.sem("hp_done")
        hT_done = f.sem("hT_done")
        op_done = f.sem("op_done")
        yb_done = f.sem("yb_done")
        resb_done = f.sem("resb_done")
        r_done = f.sem("r_done")
        stats_done = f.sem("stats_done")
        pace = f.sem("pace")
        var_done = f.sem("var_done")
        var_eps = f.sem("var_eps")
        rstd_done = f.sem("rstd_done")
        z_done = f.sem("z_done")
        scaled = f.sem("scaled")
        x1_done = f.sem("x1_done")
        xn1_done = f.sem("xn1_done")
        stored = f.sem("stored")
        turn = f.sem("turn")
        block = f.block()
        yg, rg, x1g, xn1g = tiles(y_d), tiles(res_d), tiles(x1_d), tiles(xn1_d[1:N + 1, :])

        @block.sync
        def _(sp):
            sp.sem_inc(stored, 32)
            sp.dma_start(y[:, 0, :, :], yg[0]).then_inc(loaded[0], 16)
            sp.dma_start(res[:, 0, :, :], rg[0]).then_inc(loaded[0], 16)
            sp.dma_start(w1[:, :, :], rows(w1T)).then_inc(weights, 16)
            sp.dma_start(w2[:, :, :], rows(w2T)).then_inc(weights, 16)
            sp.dma_start(b1c[:, :], b1).then_inc(weights, 16)
            sp.dma_start(b2r[:, :], spread(b2)).then_inc(weights, 16)
            sp.dma_start(gm[:, :], spread(gamma)).then_inc(weights, 16)
            sp.dma_start(bt[:, :], spread(beta)).then_inc(weights, 16)
            with sp.Fori(0, NG // 2) as i:
                for u in range(2):
                    g = 2 * i + u
                    sp.wait_ge(tr_done, 4 * g + 4)
                    sp.wait_ge(resb_done, 4 * g + 4)
                    sp.sem_inc(turn, 1)
                    sp.dma_start(y[:, 1 - u, :, :], yg[(g + 1) % NG]).then_inc(loaded[1 - u], 16)
                    sp.dma_start(res[:, 1 - u, :, :], rg[(g + 1) % NG]).then_inc(loaded[1 - u], 16)
                    sp.wait_ge(x1_done, 4 * g + 4)
                    sp.dma_start(x1g[g], x1[:, :, :]).then_inc(stored, 16)
                    sp.wait_ge(xn1_done, 4 * g + 8)
                    sp.dma_start(xn1g[g], xn1[:, :, :]).then_inc(stored, 16)
            sp.wait_ge(loaded[0], 32 * (NG // 2 + 1))
            sp.wait_ge(stored, 32 * NG + 32)

        @block.gpsimd
        def _(pool):
            pool.sem_inc(resb_done, 4)
            nc.gpsimd.memset(half[:, :], -0.5).then_inc(prepared, 1)
            nc.gpsimd.memset(eps[:, :], EPS).then_inc(prepared, 1)
            pool.wait_ge(prepared, 2)
            pool.wait_ge(weights, 96)
            with pool.Fori(0, NG // 2) as i:
                for u in range(2):
                    g = 2 * i + u
                    pool.wait_ge(loaded[u], 32 * i + 32)
                    pool.wait_ge(xn1_done, 4 * g + 4)
                    for s in range(SUB):
                        nc.gpsimd.tensor_tensor(yb[:, s, :], y[:, u, s, :], b2r[:, :], ALU.add).then_inc(yb_done, 1)
                    for s in range(SUB):
                        nc.gpsimd.tensor_tensor(resb[:, s, :], res[:, u, s, :], bt[:, :], ALU.add).then_inc(resb_done, 1)
                    for k in range(2):
                        pool.wait_ge(var_done, 8 * g + 4 * k + 4)
                        nc.gpsimd.tensor_tensor(ve[:, :], mv[:, :, 1], eps[:, :], ALU.add).then_inc(var_eps, 1)
                        pool.wait_ge(var_eps, 2 * g + k + 1)
                        nc.gpsimd.tensor_tensor(rstd[:, :], ve[:, :], half[:, :], ALU.pow).then_inc(rstd_done, 1)
                        if k == 0:
                            for s in range(SUB):
                                pool.wait_ge(z_done, 4 * g + s + 1)
                                nc.gpsimd.tensor_tensor(z[:, s, :], z[:, s, :], gm[:, :], ALU.mult).then_inc(scaled, 1)

        @block.vector
        def _(dve):
            dve.sem_inc(xn1_done, 4)
            with dve.Fori(0, NG // 2) as i:
                for u in range(2):
                    g = 2 * i + u
                    for s in range(SUB):
                        dve.wait_ge(op_done, 4 * g + s + 1)
                        dve.wait_ge(yb_done, 4 * g + s + 1)
                        nc.vector.tensor_tensor(r[:, s, :], op[:, s % 2, 0:D], yb[:, s, :], ALU.add).then_inc(r_done, 1)
                    for s in range(SUB):
                        dve.wait_ge(r_done, 4 * g + s + 1)
                        nc.vector.bn_stats(stats[:, s, :], r[:, s, :]).then_inc(stats_done, 1)
                    dve.wait_ge(stats_done, 8 * g + 4)
                    dve.sem_inc(pace, 1)
                    for s in range(SUB):
                        nc.vector.bn_aggr(mv[:, s, :], stats[:, s, :]).then_inc(var_done, 1)
                    dve.wait_ge(var_done, 8 * g + 4)
                    dve.wait_ge(rstd_done, 2 * g + 1)
                    for s in range(SUB):
                        nc.vector.tensor_scalar(z[:, s, :], r[:, s, :], mv[:, s, 0:1], rstd[:, s:s + 1],
                                                ALU.subtract, ALU.mult).then_inc(z_done, 1)
                    dve.wait_ge(stored, 32 * g + 32)
                    for s in range(SUB):
                        dve.wait_ge(scaled, 4 * g + s + 1)
                        dve.wait_ge(resb_done, 4 * g + s + 5)
                        nc.vector.tensor_tensor(x1[:, s, :], z[:, s, :], resb[:, s, :], ALU.add).then_inc(x1_done, 1)
                    for s in range(SUB):
                        dve.wait_ge(x1_done, 4 * g + s + 1)
                        nc.vector.bn_stats(stats[:, s, :], x1[:, s, :]).then_inc(stats_done, 1)
                    dve.wait_ge(stats_done, 8 * g + 8)
                    dve.sem_inc(pace, 1)
                    for s in range(SUB):
                        nc.vector.bn_aggr(mv[:, s, :], stats[:, s, :]).then_inc(var_done, 1)
                    dve.wait_ge(var_done, 8 * g + 8)
                    dve.wait_ge(rstd_done, 2 * g + 2)
                    for s in range(SUB):
                        nc.vector.tensor_scalar(xn1[:, s, :], x1[:, s, :], mv[:, s, 0:1], rstd[:, s:s + 1],
                                                ALU.subtract, ALU.mult).then_inc(xn1_done, 1)

        @block.scalar
        def _(act):
            act.wait_ge(weights, 96)
            with act.Fori(0, NG // 2) as i:
                for u in range(2):
                    g = 2 * i + u
                    for s in range(SUB):
                        act.wait_ge(tr_done, 4 * g + s + 1)
                        nc.scalar.activation(yT[:, :, P * s:P * s + P], tr[:, s % 2, 0:D].rearrange("p (c n) -> p c n", c=DC),
                                             ACT.Copy).then_inc(yT_done, 1)
                    for c in range(FC):
                        act.wait_ge(hp_done, FC * g + c + 1)
                        nc.scalar.activation(hT[:, c, :], hp[:, c % 4, :], ACT.Gelu, bias=b1c[:, c:c + 1]).then_inc(hT_done, 1)

        @block.tensor
        def _(pe):
            pe.wait_ge(weights, 96)
            with pe.Fori(0, NG // 2) as i:
                for u in range(2):
                    g = 2 * i + u
                    pe.wait_ge(loaded[u], 32 * i + 32)
                    for s in range(SUB):
                        if s >= 2:
                            pe.wait_ge(yT_done, 4 * g + s - 1)
                        for c in range(DC):
                            last = nc.tensor.transpose(tr[:, s % 2, P * c:P * c + P], y[:, u, s, P * c:P * c + P], ident[:, :])
                        last.then_inc(tr_done, 1)
                    pe.wait_ge(yT_done, 4 * g + 4)
                    for m in range(FC):
                        if m >= 4:
                            pe.wait_ge(hT_done, FC * g + m - 3)
                        for c in range(DC):
                            last = nc.tensor.matmul(hp[:, m % 4, :], w1[:, c, P * m:P * m + P], yT[:, c, :],
                                                    start=c == 0, stop=c == DC - 1)
                        last.then_inc(hp_done, 1)
                    for s in range(SUB):
                        pe.wait_ge(hT_done, FC * g + FC)
                        if s >= 2:
                            pe.wait_ge(r_done, 4 * g + s - 1)
                        else:
                            pe.wait_ge(xn1_done, 4 * g + 4)
                        for c in range(FC):
                            last = nc.tensor.matmul(op[:, s % 2, 0:D], hT[:, c, P * s:P * s + P], w2[:, c, :],
                                                    start=c == 0, stop=c == FC - 1)
                        last.then_inc(op_done, 1)


H1 = 16
HD1 = D // H1
LAT = 64
ROPE = 128
PARTS = 3
VC = PARTS * HD1 + 1


TINY = 1e-15


def latent_projections(nc, a, cos_t, sin_t, ident, xn1_d, qk_d, v_d):
    with Frame(nc, "latent") as f:
        wc = f.sb("wc", [P, DC, 2 * LAT])
        wr = f.sb("wr", [P, DC, 4, ROPE])
        wu = f.sb("wu", [2 * LAT, ROPE])
        wv = f.sb("wv", [2 * LAT, D])
        bc = f.sb("bc", [P, 1])
        bu = f.sb("bu", [P, 2])
        br = f.sb("br", [P, 4])
        bv = f.sb("bv", [P, D])
        cos = f.sb("cos", [P, 2, GROUP])
        sin = f.sb("sin", [P, 2, GROUP])
        xin = f.sb("xin", [P, 2, SUB, D])
        xT = f.sb("xT", [P, DC, GROUP])
        cT = f.sb("cT", [P, GROUP])
        turned = f.sb("turned", [P, 4, GROUP])
        rope = f.sb("rope", [P, 2, GROUP])
        raw = f.sb("raw", [P, 4, GROUP])
        low = f.sb("low", [P, 4, GROUP])
        qk = f.sb("qk", [P, 4, GROUP])
        rest = f.sb("rest", [P, 4, GROUP])
        part = f.sb("part", [P, 4, PARTS, GROUP], BF16)
        v = f.sb("v", [P, SUB, D])
        vrest = f.sb("vrest", [P, SUB, D])
        vpart = f.sb("vpart", [P, H1, SUB, VC], BF16)
        tr = f.psum("tr", [P, 2, 512])
        cp = f.psum("cp", [P, 512])
        rp = f.psum("rp", [P, 2, 512])
        up = f.psum("up", [P, 512])
        vp = f.psum("vp", [P, 2, 512])

        weights = f.sem("weights")
        prepared = f.sem("prepared")
        loaded = [f.sem(f"loaded{u}") for u in range(2)]
        tr_done = f.sem("tr_done")
        xT_done = f.sem("xT_done")
        cp_done = f.sem("cp_done")
        cT_done = f.sem("cT_done")
        rp_done = f.sem("rp_done")
        turned_done = f.sem("turned_done")
        rope_done = f.sem("rope_done")
        up_done = f.sem("up_done")
        raw_done = f.sem("raw_done")
        low_done = f.sem("low_done")
        qk_done = f.sem("qk_done")
        first_done = f.sem("first_done")
        rest_done = f.sem("rest_done")
        second_done = f.sem("second_done")
        third_done = f.sem("third_done")
        vp_done = f.sem("vp_done")
        v_done = f.sem("v_done")
        v_first = f.sem("v_first")
        v_rest = f.sem("v_rest")
        v_second = f.sem("v_second")
        v_third = f.sem("v_third")
        stored = f.sem("stored")
        turn = f.sem("turn")
        block = f.block()
        xg = tiles(xn1_d[1:N + 1, :])
        qkg = qk_d.rearrange("o a (r p) (g n) -> g o r p a n", p=P, n=GROUP)
        cosg = cos_t.rearrange("p (g n) -> g p n", n=GROUP)
        sing = sin_t.rearrange("p (g n) -> g p n", n=GROUP)

        def column(b):
            return b.rearrange("(n a) -> n a", a=1)

        @block.sync
        def _(sp):
            sp.sem_inc(stored, 80)
            sp.dma_start(xin[:, 0, :, :], xg[0]).then_inc(loaded[0], 16)
            sp.dma_start(cos[:, 0, :], cosg[0]).then_inc(loaded[0], 16)
            sp.dma_start(sin[:, 0, :], sing[0]).then_inc(loaded[0], 16)
            sp.dma_start(wc[:, :, 0:LAT], rows(a["L1_attn_wq"])).then_inc(weights, 16)
            sp.dma_start(wc[:, :, LAT:2 * LAT], rows(a["L1_attn_wkv"])).then_inc(weights, 16)
            h = ROPE // 2
            for k, (w, b) in enumerate((("L1_attn_wqr", "L1_attn_bqr"), ("L1_attn_wkr", "L1_attn_bkr"))):
                sp.dma_start(wr[:, :, 2 * k, :], rows(a[w])).then_inc(weights, 16)
                sp.dma_start(wr[:, :, 2 * k + 1, 0:h], rows(a[w][:, h:ROPE])).then_inc(weights, 16)
                sp.dma_start(wr[:, :, 2 * k + 1, h:ROPE], rows(a[w][:, 0:h])).then_inc(weights, 16)
                sp.dma_start(br[:, 2 * k:2 * k + 1], column(a[b])).then_inc(weights, 16)
                sp.dma_start(br[0:h, 2 * k + 1:2 * k + 2], column(a[b][h:ROPE])).then_inc(weights, 16)
                sp.dma_start(br[h:ROPE, 2 * k + 1:2 * k + 2], column(a[b][0:h])).then_inc(weights, 16)
            sp.dma_start(wu[0:LAT, :], a["L1_attn_wqc"]).then_inc(weights, 16)
            sp.dma_start(wu[LAT:2 * LAT, :], a["L1_attn_wkc"]).then_inc(weights, 16)
            sp.dma_start(wv[LAT:2 * LAT, :], a["L1_attn_wv"]).then_inc(weights, 16)
            sp.dma_start(bc[0:LAT, :], column(a["L1_attn_bq"])).then_inc(weights, 16)
            sp.dma_start(bc[LAT:2 * LAT, :], column(a["L1_attn_bkv"])).then_inc(weights, 16)
            sp.dma_start(bu[:, 0:1], column(a["L1_attn_bqc"])).then_inc(weights, 16)
            sp.dma_start(bu[:, 1:2], column(a["L1_attn_bkc"])).then_inc(weights, 16)
            sp.dma_start(bv[:, :], spread(a["L1_attn_bv"])).then_inc(weights, 16)
            with sp.Fori(0, NG // 2) as i:
                for u in range(2):
                    g = 2 * i + u
                    sp.wait_ge(tr_done, 4 * g + 4)
                    sp.wait_ge(turned_done, 4 * g + 4)
                    sp.sem_inc(turn, 1)
                    sp.dma_start(xin[:, 1 - u, :, :], xg[(g + 1) % NG]).then_inc(loaded[1 - u], 16)
                    sp.dma_start(cos[:, 1 - u, :], cosg[(g + 1) % NG]).then_inc(loaded[1 - u], 16)
                    sp.dma_start(sin[:, 1 - u, :], sing[(g + 1) % NG]).then_inc(loaded[1 - u], 16)
                    for k in range(4):
                        sp.wait_ge(third_done, 4 * g + k + 1)
                        sp.sem_inc(turn, 1)
                        sp.dma_start(qkg[g, k % 2, k // 2], part[:, k, :, :]).then_inc(stored, 16)
                    sp.wait_ge(v_third, g + 1)
                    sp.dma_start(v_d[g], vpart[:, :, :, :]).then_inc(stored, 16)
            sp.wait_ge(loaded[0], 48 * (NG // 2 + 1))
            sp.wait_ge(stored, 80 * NG + 80)

        heads = "p s (h d) -> p h s d"

        @block.gpsimd
        def _(pool):
            nc.gpsimd.memset(vpart[:, :, :, :], 1.0).then_inc(prepared, 1)
            pool.wait_ge(prepared, 1)
            with pool.Fori(0, NG) as g:
                for k in range(4):
                    pool.wait_ge(first_done, 4 * g + k + 1)
                    nc.gpsimd.tensor_tensor(rest[:, k, :], qk[:, k, :], part[:, k, 0, :], ALU.subtract).then_inc(rest_done, 1)
                for k in range(4):
                    pool.wait_ge(second_done, 4 * g + k + 1)
                    nc.gpsimd.tensor_tensor(part[:, k, 2, :], rest[:, k, :], part[:, k, 1, :], ALU.subtract).then_inc(third_done, 1)

        @block.vector
        def _(dve):
            dve.sem_inc(turned_done, 4)
            dve.wait_ge(weights, 16 * 22)
            dve.wait_ge(prepared, 1)
            with dve.Fori(0, NG // 2) as i:
                for u in range(2):
                    g = 2 * i + u
                    dve.wait_ge(loaded[u], 48 * i + 48)
                    for k in range(4):
                        dve.wait_ge(rp_done, 4 * g + k + 1)
                        table = cos if k % 2 == 0 else sin
                        nc.vector.scalar_tensor_tensor(turned[:, k, :], rp[:, k % 2, :], br[:, k:k + 1], table[:, u, :],
                                                       ALU.add, ALU.mult).then_inc(turned_done, 1)
                    for k in range(2):
                        dve.wait_ge(turned_done, 4 * g + 2 * k + 6)
                        nc.vector.tensor_tensor(rope[:, k, :], turned[:, 2 * k, :], turned[:, 2 * k + 1, :], ALU.add).then_inc(rope_done, 1)
                    for s in range(SUB):
                        dve.wait_ge(vp_done, 4 * g + s + 1)
                        nc.vector.tensor_tensor(v[:, s, :], vp[:, s % 2, 0:D], bv[:, :], ALU.add).then_inc(v_done, 1)
                    dve.wait_ge(v_done, 4 * g + 4)
                    dve.wait_ge(stored, 80 * g + 80)
                    for k in range(4):
                        dve.wait_ge(raw_done, 4 * g + k + 1)
                        nc.vector.scalar_tensor_tensor(low[:, k, :], raw[:, k, :], -TINY, raw[:, k, :],
                                                       ALU.is_le, ALU.mult).then_inc(low_done, 1)
                    for k in range(4):
                        dve.wait_ge(low_done, 4 * g + k + 1)
                        nc.vector.tensor_tensor(qk[:, k, :], low[:, k, :], raw[:, k, :], ALU.max).then_inc(qk_done, 1)
                    for s in range(SUB):
                        last = nc.vector.tensor_copy(vpart[:, :, s, 0:HD1], v[:, s, :].rearrange("p (h d) -> p h d", d=HD1))
                    last.then_inc(v_first, 1)
                    dve.wait_ge(v_first, g + 1)
                    for s in range(SUB):
                        last = nc.vector.tensor_tensor(vrest[:, s, :].rearrange("p (h d) -> p h d", d=HD1),
                                                       v[:, s, :].rearrange("p (h d) -> p h d", d=HD1),
                                                       vpart[:, :, s, 0:HD1], ALU.subtract)
                    last.then_inc(v_rest, 1)
                    dve.wait_ge(v_rest, g + 1)
                    for s in range(SUB):
                        last = nc.vector.tensor_copy(vpart[:, :, s, HD1:2 * HD1], vrest[:, s, :].rearrange("p (h d) -> p h d", d=HD1))
                    last.then_inc(v_second, 1)
                    dve.wait_ge(v_second, g + 1)
                    for s in range(SUB):
                        last = nc.vector.tensor_tensor(vpart[:, :, s, 2 * HD1:3 * HD1],
                                                       vrest[:, s, :].rearrange("p (h d) -> p h d", d=HD1),
                                                       vpart[:, :, s, HD1:2 * HD1], ALU.subtract)
                    last.then_inc(v_third, 1)

        @block.scalar
        def _(act):
            act.wait_ge(weights, 16 * 22)
            with act.Fori(0, NG // 2) as i:
                for u in range(2):
                    g = 2 * i + u
                    for s in range(SUB):
                        act.wait_ge(tr_done, 4 * g + s + 1)
                        nc.scalar.activation(xT[:, :, P * s:P * s + P], tr[:, s % 2, 0:D].rearrange("p (c n) -> p c n", c=DC),
                                             ACT.Copy).then_inc(xT_done, 1)
                    act.wait_ge(cp_done, g + 1)
                    nc.scalar.activation(cT[:, :], cp[:, :], ACT.Gelu, bias=bc[:, :]).then_inc(cT_done, 1)
                    act.wait_ge(stored, 80 * g + 80)
                    for k in range(4):
                        if k < 2:
                            act.wait_ge(up_done, 2 * g + k + 1)
                            nc.scalar.activation(raw[:, k, :], up[:, :], ACT.Gelu, bias=bu[:, k:k + 1]).then_inc(raw_done, 1)
                        else:
                            act.wait_ge(rope_done, 2 * g + k - 1)
                            nc.scalar.activation(raw[:, k, :], rope[:, k - 2, :], ACT.Gelu).then_inc(raw_done, 1)
                    for k in range(4):
                        act.wait_ge(qk_done, 4 * g + k + 1)
                        nc.scalar.activation(part[:, k, 0, :], qk[:, k, :], ACT.Copy).then_inc(first_done, 1)
                    for k in range(4):
                        act.wait_ge(rest_done, 4 * g + k + 1)
                        nc.scalar.activation(part[:, k, 1, :], rest[:, k, :], ACT.Copy).then_inc(second_done, 1)

        @block.tensor
        def _(pe):
            pe.wait_ge(weights, 16 * 22)
            with pe.Fori(0, NG // 2) as i:
                for u in range(2):
                    g = 2 * i + u
                    pe.wait_ge(loaded[u], 48 * i + 48)
                    for s in range(SUB):
                        if s >= 2:
                            pe.wait_ge(xT_done, 4 * g + s - 1)
                        for c in range(DC):
                            last = nc.tensor.transpose(tr[:, s % 2, P * c:P * c + P], xin[:, u, s, P * c:P * c + P], ident[:, :])
                        last.then_inc(tr_done, 1)
                    pe.wait_ge(xT_done, 4 * g + 4)
                    for c in range(DC):
                        last = nc.tensor.matmul(cp[:, :], wc[:, c, :], xT[:, c, :], start=c == 0, stop=c == DC - 1)
                    last.then_inc(cp_done, 1)
                    for k in range(4):
                        pe.wait_ge(turned_done, 4 * g + k + 3)
                        for c in range(DC):
                            last = nc.tensor.matmul(rp[:, k % 2, :], wr[:, c, k, :], xT[:, c, :], start=c == 0, stop=c == DC - 1)
                        last.then_inc(rp_done, 1)
                    pe.wait_ge(cT_done, g + 1)
                    for k in range(2):
                        if k:
                            pe.wait_ge(raw_done, 4 * g + k)
                        half = slice(LAT * k, LAT * k + LAT)
                        nc.tensor.matmul(up[:, :], wu[half, :], cT[half, :], start=True, stop=True).then_inc(up_done, 1)
                    for s in range(SUB):
                        if s >= 2:
                            pe.wait_ge(v_done, 4 * g + s - 1)
                        nc.tensor.matmul(vp[:, s % 2, 0:D], cT[LAT:2 * LAT, P * s:P * s + P], wv[LAT:2 * LAT, :],
                                         start=True, stop=True).then_inc(vp_done, 1)


PAIR_Q = (0, 0, 1, 1, 0, 2)
PAIR_K = (0, 1, 0, 1, 2, 0)
DEPTH = HD1 * len(PAIR_Q)
FULL = DEPTH + PARTS
UNIT = 1024
SCAN = 512


def score_units():
    units = []
    for c in range(NG):
        for k in range(0, SUB * c, 2):
            units.append((c, [(k, 0, 0, GROUP, False), (k + 1, 0, GROUP, GROUP, False)]))
        k = SUB * c
        units.append((c, [(k, 0, 0, GROUP, True), (k + 1, P, GROUP, GROUP - P, True)]))
        units.append((c, [(k + 2, 2 * P, 0, 2 * P, True), (k + 3, 3 * P, 2 * P, P, True)]))
    return units


def max_units():
    return [(i, k, min(SCAN, P * (i + 1) - k), k + SCAN >= P * (i + 1))
            for i in range(NT) for k in range(0, P * (i + 1), SCAN)]


def high(x):
    return x.bitcast(BF16).rearrange("p (n two) -> p n two", two=2)[:, :, 1]


def latent_attention(nc, sel_d, ident, identb, causal_q, causal_k, qk_d, v_d, o_d):
    units, maxima = score_units(), max_units()
    NU, NM = len(units), len(maxima)
    last_of = {c: max(n for n, (d, _) in enumerate(units) if d == c) for c in range(NG)}
    first_of = {c: min(n for n, (d, _) in enumerate(units) if d == c) for c in range(NG)}
    ends = {n: c for c, n in last_of.items()}
    BEGIN, END = 7, NU - 7
    due = [0 if n < BEGIN else min(NM, (n - BEGIN + 1) * NM // (END - BEGIN) + 1) for n in range(NU)]
    TURN = END + 4
    on_pool = [n % 3 != 2 for n in range(NU)]
    PER_POOL = sum(on_pool)
    PER_DVE = NU - PER_POOL
    LOADS = 16 * (2 * len(PAIR_Q) + 1)
    pool_until = [sum(on_pool[:n + 1]) for n in range(NU)]
    RING = 6
    LAG = 3
    with Frame(nc, "mla") as f:
        qs = f.sb("qs", [P, 2, N], BF16)
        ks = f.sb("ks", [P, 2, N], BF16)
        vs = f.sb("vs", [P, 2, NT, VC], BF16)
        prob = f.sb("prob", [P, RING, UNIT])
        low = f.sb("low", [P, RING, UNIT], BF16)
        mpart = f.sb("mpart", [P, NT, N // SCAN])
        peak = f.sb("peak", [P, NT])
        neg = f.sb("neg", [P, NT])
        nrest = f.sb("nrest", [P, NT])
        mrow = f.sb("mrow", [P, PARTS, NT], BF16)
        mrowT = f.sb("mrowT", [PARTS * NT, P], BF16)
        oT = f.sb("oT", [VC, 2, GROUP])
        sel = f.sb("sel", [VC, VW])
        rec = f.sb("rec", [P, 2, SUB])
        ao = f.sb("ao", [P, NT, D])
        score_banks = [f.psum(f"scores{b}", [P, UNIT]) for b in range(2)]
        mx = f.psum("mx", [P, 2, 512])
        op = f.psum("op", [P, 2, 512])

        cleared = f.sem("cleared")
        sel_loaded = f.sem("sel_loaded")
        stacks = [f.sem(f"stacks{u}") for u in range(2)]
        mx_done = f.sem("mx_done")
        mx_read = f.sem("mx_read")
        peak_done = f.sem("peak_done")
        neg_done = f.sem("neg_done")
        m_first = f.sem("m_first")
        m_rest = f.sem("m_rest")
        m_second = f.sem("m_second")
        m_third = f.sem("m_third")
        turned = f.sem("turned")
        turned_read = f.sem("turned_read")
        mrows = [f.sem(f"mrows{u}") for u in range(2)]
        s_done = f.sem("s_done")
        p_done = f.sem("p_done")
        low_dve = f.sem("low_dve")
        low_pool = f.sem("low_pool")
        pv_done = f.sem("pv_done")
        oT_done = f.sem("oT_done")
        out_done = f.sem("out_done")
        rec_done = f.sem("rec_done")
        ao_done = f.sem("ao_done")
        turn = f.sem("turn")
        stored = f.sem("stored")
        block = f.block()
        qkh = qk_d.rearrange("o a (h d) n -> h o a d n", d=HD1)
        vh = v_d.rearrange("g p h s w -> h p g (s w)")

        @block.sync
        def _(sp):
            sp.dma_start(sel[:, :], sel_d).then_inc(sel_loaded, 16)

            def load(h, u):
                for r, (a, b) in enumerate(zip(PAIR_Q, PAIR_K)):
                    sp.dma_start(ks[HD1 * r:HD1 * r + HD1, u, :], qkh[h, 1, b]).then_inc(stacks[u], 16)
                    sp.dma_start(qs[HD1 * r:HD1 * r + HD1, u, :], qkh[h, 0, a]).then_inc(stacks[u], 16)
                sp.dma_start(vs[:, u, :, :].rearrange("p (g s) w -> p g (s w)", s=SUB), vh[h]).then_inc(stacks[u], 16)

            def load_maxima(h, u):
                sp.wait_ge(turned_read, h + 1)
                for a in range(PARTS):
                    sp.dma_start(qs[DEPTH + a:DEPTH + a + 1, u, :].rearrange("a (t n) -> a t n", n=P),
                                 mrowT[NT * a:NT * a + NT, :]).then_inc(mrows[u], 16)

            def pair(i, more):
                load_maxima(2 * i + 1, 1)
                if more:
                    sp.wait_ge(pv_done, NU * (2 * i + 1) + RING)
                    sp.sem_inc(turn, 1)
                    load(2 * i + 2, 0)
                    load_maxima(2 * i + 2, 0)
                    sp.wait_ge(pv_done, NU * (2 * i + 2) + RING)
                    sp.sem_inc(turn, 1)
                    load(2 * i + 3, 1)

            load(0, 0)
            load(1, 1)
            load_maxima(0, 0)
            with sp.Fori(0, H1 // 2 - 1) as i:
                pair(i, True)
            pair(H1 // 2 - 1, False)
            sp.wait_ge(ao_done, NG * H1 + 2)
            sp.dma_start(o_d.rearrange("(t p) d -> p t d", p=P), ao[:, :, :]).then_inc(stored, 16)
            sp.wait_ge(stored, 16)

        @block.gpsimd
        def _(pool):
            nc.gpsimd.memset(ks[DEPTH:P, :, :], 1.0).then_inc(cleared, 1)
            pool.wait_ge(cleared, 1)
            nc.gpsimd.memset(mpart[:, :, :], -3e38).then_inc(cleared, 1)

            def pair(i):
                for u in range(2):
                    h = 2 * i + u
                    for n in range(NU):
                        if on_pool[n]:
                            pool.wait_ge(p_done, NU * h + n + 3)
                            pool.wait_ge(pv_done, NU * h + n + 1)
                            w = units[n][1][1][2] + units[n][1][1][3]
                            x = prob[:, n % RING, 0:w]
                            nc.gpsimd.tensor_tensor(low[:, n % RING, 0:w], x, high(x), ALU.subtract).then_inc(low_pool, 1)

            with pool.Fori(0, H1 // 2) as i:
                pair(i)

        @block.vector
        def _(dve):
            dve.wait_ge(cleared, 2)
            dve.sem_inc(ao_done, 2)

            def reduce(h, m):
                i, k, w, _ = maxima[m]
                dve.wait_ge(mx_done, NM * h + m + 1)
                nc.vector.tensor_reduce(mpart[:, i, k // SCAN:k // SCAN + 1], mx[:, m % 2, 0:w], AX.X, ALU.max).then_inc(mx_read, 1)

            def split_maxima(h):
                dve.wait_ge(mx_read, NM * (h + 1) + h + 1)
                nc.vector.tensor_reduce(peak[:, :], mpart[:, :, :], AX.X, ALU.max).then_inc(peak_done, 1)
                dve.wait_ge(peak_done, h + 1)
                nc.vector.tensor_scalar(neg[:, :], peak[:, :], -1.0, None, ALU.mult).then_inc(neg_done, 1)
                dve.wait_ge(neg_done, h + 1)
                nc.vector.tensor_copy(mrow[:, 0, :], neg[:, :]).then_inc(m_first, 1)
                dve.wait_ge(m_first, h + 1)
                nc.vector.tensor_tensor(nrest[:, :], neg[:, :], mrow[:, 0, :], ALU.subtract).then_inc(m_rest, 1)
                dve.wait_ge(m_rest, h + 1)
                nc.vector.tensor_copy(mrow[:, 1, :], nrest[:, :]).then_inc(m_second, 1)
                dve.wait_ge(m_second, h + 1)
                nc.vector.tensor_tensor(mrow[:, 2, :], nrest[:, :], mrow[:, 1, :], ALU.subtract).then_inc(m_third, 1)

            def take_rows(h, i=None, u=None):
                if u is not None:
                    dve.wait_ge(mrows[u], 16 * PARTS * i + 16 * PARTS)
                dve.wait_ge(turned, h + 1)
                nc.vector.tensor_copy(mrowT[:, :], mx[:, 0, :].bitcast(BF16)[0:PARTS * NT, 0:P]).then_inc(turned_read, 1)
                dve.wait_ge(turned_read, h + 1)
                dve.sem_inc(mx_read, 1)

            def finish(h, c):
                o = op[:, c % 2, 0:SUB * VW].rearrange("p (s w) -> p s w", w=VW)
                dve.wait_ge(out_done, NG * h + c + 1)
                nc.vector.reciprocal(rec[:, c % 2, :], o[:, :, HD1]).then_inc(rec_done, 1)
                dve.wait_ge(rec_done, NG * h + c + 1)
                nc.vector.tensor_tensor(ao[:, SUB * c:SUB * c + SUB, bass.ds(h * HD1, HD1)], o[:, :, 0:HD1],
                                        rec[:, c % 2, :].unsqueeze(2).broadcast_to([P, SUB, HD1]), ALU.mult).then_inc(ao_done, 1)

            for m in range(NM):
                reduce(0, m)
            split_maxima(0)
            take_rows(0)

            def pair(i, more):
                for step in range(2 * NU + LAG + 2):
                    u, n = divmod(step, NU)
                    if step < 2 * NU:
                        h = 2 * i + u
                        scans = list(range(due[n - 1] if n else 0, due[n])) if u == 0 or more else []
                        for m in scans[:2]:
                            reduce(h + 1, m)
                    if 1 <= step <= 2 * NU:
                        back, b = divmod(step - 1, NU)
                        if not on_pool[b]:
                            dve.wait_ge(p_done, NU * (2 * i + back) + b + 3)
                            dve.wait_ge(pv_done, NU * (2 * i + back) + b + 1)
                            w = units[b][1][1][2] + units[b][1][1][3]
                            p = prob[:, b % RING, 0:w]
                            nc.vector.tensor_tensor(low[:, b % RING, 0:w], p, high(p), ALU.subtract).then_inc(low_dve, 1)
                    if step < 2 * NU:
                        if u == 0 or more:
                            for m in scans[2:]:
                                reduce(h + 1, m)
                            if n == END:
                                split_maxima(h + 1)
                            if n == TURN:
                                take_rows(h + 1, i, u)
                    back = step - LAG - 2
                    if 0 <= back < 2 * NU and back % NU in ends:
                        finish(2 * i + back // NU, ends[back % NU])

            with dve.Fori(0, H1 // 2 - 1) as i:
                pair(i, True)
            pair(H1 // 2 - 1, False)

        @block.scalar
        def _(act):
            act.sem_inc(p_done, 2)

            def pair(i):
                for step in range(2 * NU + LAG + 1):
                    u, n = divmod(step, NU)
                    if step < 2 * NU:
                        h = 2 * i + u
                        w = units[n][1][1][2] + units[n][1][1][3]
                        act.wait_ge(s_done, NU * h + n + 1)
                        act.wait_ge(pv_done, NU * h + n + 1)
                        nc.scalar.activation(prob[:, n % RING, 0:w], score_banks[n % 2][:, 0:w], ACT.Exp,
                                             scale=float(HD1) ** -0.5).then_inc(p_done, 1)
                    back = step - LAG
                    if 0 <= back < 2 * NU and back % NU in ends:
                        c = ends[back % NU]
                        act.wait_ge(pv_done, NU * (2 * i + back // NU) + last_of[c] + 1 + RING)
                        nc.scalar.activation(oT[:, c % 2, :], op[0:VC, c % 2, :], ACT.Copy).then_inc(oT_done, 1)

            with act.Fori(0, H1 // 2) as i:
                pair(i)

        @block.tensor
        def _(pe):
            pe.sem_inc(mx_read, 1)
            pe.sem_inc(pv_done, RING)
            pe.wait_ge(sel_loaded, 16)

            def scan(h, u, m):
                i, k, w, diagonal = maxima[m]
                pe.wait_ge(mx_read, NM * h + h + max(m - 1, 0) + 1)
                last = nc.tensor.matmul(mx[:, m % 2, 0:w], qs[0:DEPTH, u, P * i:P * i + P], ks[0:DEPTH, u, k:k + w],
                                        start=True, stop=not diagonal)
                if diagonal:
                    last = nc.tensor.matmul(mx[:, m % 2, w - P:w], identb[:, :], causal_q[:, :], start=False, stop=True)
                last.then_inc(mx_done, 1)

            def turn_maxima(h):
                pe.wait_ge(m_third, h + 1)
                nc.tensor.transpose(mx[:, 0, :].bitcast(BF16)[0:PARTS * NT, 0:P], mrow[:, :, :].rearrange("p a t -> p (a t)"),
                                    identb[:, :]).then_inc(turned, 1)

            def score(h, u, n):
                c, parts = units[n]
                pe.wait_ge(p_done, NU * h + n + 1)
                for k, q0, col, w, diagonal in parts:
                    last = nc.tensor.matmul(score_banks[n % 2][:, col:col + w], ks[0:FULL, u, P * k:P * k + P],
                                            qs[0:FULL, u, GROUP * c + q0:GROUP * c + GROUP], start=True, stop=not diagonal)
                    if diagonal:
                        last = nc.tensor.matmul(score_banks[n % 2][:, col:col + P], identb[:, :], causal_k[:, :], start=False, stop=True)
                last.then_inc(s_done, 1)

            def weigh(h, u, n, j):
                c, parts = units[n]
                if j == 0 and n == first_of[c]:
                    pe.wait_ge(ao_done, NG * h + c + 1)
                if j == 0 and on_pool[n]:
                    pe.wait_ge(low_pool, PER_POOL * h + pool_until[n])
                elif j == 0:
                    pe.wait_ge(low_dve, PER_DVE * h + n + 1 - pool_until[n])
                k, q0, col, w, _ = parts[j]
                nc.tensor.matmul(op[0:VC, c % 2, q0:q0 + w], vs[:, u, k, :], high(prob[:, n % RING, col:col + w]),
                                 start=n == first_of[c] and j == 0, stop=False)
                last = nc.tensor.matmul(op[0:VC, c % 2, q0:q0 + w], vs[:, u, k, :], low[:, n % RING, col:col + w],
                                        start=False, stop=n == last_of[c] and j == 1)
                if j == 1:
                    last.then_inc(pv_done, 1)

            def gather(h, c):
                pe.wait_ge(oT_done, NG * h + c + 1)
                for s in range(SUB):
                    last = nc.tensor.matmul(op[:, c % 2, VW * s:VW * s + VW], oT[:, c % 2, P * s:P * s + P], sel[:, :],
                                            start=True, stop=True, skip_group_check=True)
                last.then_inc(out_done, 1)

            pe.wait_ge(cleared, 2)
            pe.wait_ge(stacks[0], LOADS)
            for m in range(NM):
                scan(0, 0, m)
            turn_maxima(0)

            def pair(i, more):
                for step in range(2 * NU + LAG + 2):
                    u, n = divmod(step, NU)
                    scans = []
                    if step < 2 * NU:
                        h = 2 * i + u
                        if n == 0:
                            pe.wait_ge(mrows[u], 16 * PARTS * i + 16 * PARTS)
                            pe.wait_ge(stacks[u], LOADS * i + LOADS)
                        score(h, u, n)
                        if u == 0 or more:
                            if n == BEGIN:
                                pe.wait_ge(stacks[1 - u], LOADS * (i + u) + LOADS)
                            scans = list(range(due[n - 1] if n else 0, due[n]))
                            if n == END + 2:
                                turn_maxima(h + 1)
                    back = step - LAG
                    for j in range(max(2, len(scans))):
                        if j < len(scans):
                            scan(h + 1, 1 - u, scans[j])
                        if j < 2 and 0 <= back < 2 * NU:
                            weigh(2 * i + back // NU, back // NU, back % NU, j)
                    back = step - LAG - 2
                    if 0 <= back < 2 * NU and back % NU in ends:
                        gather(2 * i + back // NU, ends[back % NU])

            with pe.Fori(0, H1 // 2 - 1) as i:
                pair(i, True)
            pair(H1 // 2 - 1, False)


def latent_output(nc, wo_d, bo_d, ident, o_d, x1_d, sum_d):
    with Frame(nc, "lout") as f:
        wo = f.sb("wo", [P, DC, D])
        bo = f.sb("bo", [P, D])
        o = f.sb("o", [P, 2, SUB, D])
        x1 = f.sb("x1", [P, 2, SUB, D])
        xb = f.sb("xb", [P, 2, SUB, D])
        oT = f.sb("oT", [P, 2, DC, P])
        y = f.sb("y", [P, 2, SUB, D])
        tr = f.psum("tr", [P, 2, 512])
        yp = f.psum("yp", [P, 2, 512])
        weights = f.sem("weights")
        loaded = [f.sem(f"loaded{u}") for u in range(2)]
        xb_done = f.sem("xb_done")
        tr_done = f.sem("tr_done")
        oT_done = f.sem("oT_done")
        yp_done = f.sem("yp_done")
        y_done = f.sem("y_done")
        turn = f.sem("turn")
        stored = [f.sem(f"stored{u}") for u in range(2)]
        block = f.block()
        og, xg, yg = tiles(o_d), tiles(x1_d), tiles(sum_d)

        @block.sync
        def _(sp):
            for u in range(2):
                sp.sem_inc(stored[u], 16)
            sp.dma_start(o[:, 0, :, :], og[0]).then_inc(loaded[0], 16)
            sp.dma_start(x1[:, 0, :, :], xg[0]).then_inc(loaded[0], 16)
            sp.dma_start(wo[:, :, :], rows(wo_d)).then_inc(weights, 16)
            sp.dma_start(bo[:, :], spread(bo_d)).then_inc(weights, 16)
            with sp.Fori(0, NG // 2) as i:
                for u in range(2):
                    g = 2 * i + u
                    sp.wait_ge(y_done, 4 * g + 4)
                    sp.sem_inc(turn, 1)
                    sp.dma_start(o[:, 1 - u, :, :], og[(g + 1) % NG]).then_inc(loaded[1 - u], 16)
                    sp.dma_start(x1[:, 1 - u, :, :], xg[(g + 1) % NG]).then_inc(loaded[1 - u], 16)
                    sp.wait_ge(y_done, 4 * g + 8)
                    sp.dma_start(yg[g], y[:, u, :, :]).then_inc(stored[u], 16)
            sp.wait_ge(loaded[0], 32 * (NG // 2 + 1))
            for u in range(2):
                sp.wait_ge(stored[u], 16 + 16 * (NG // 2))

        @block.gpsimd
        def _(pool):
            pool.wait_ge(weights, 32)
            with pool.Fori(0, NG // 2) as i:
                for u in range(2):
                    pool.wait_ge(loaded[u], 32 * i + 32)
                    for s in range(SUB):
                        nc.gpsimd.tensor_tensor(xb[:, u, s, :], x1[:, u, s, :], bo[:, :], ALU.add).then_inc(xb_done, 1)

        @block.vector
        def _(dve):
            dve.sem_inc(y_done, 4)
            with dve.Fori(0, NG // 2) as i:
                for u in range(2):
                    g = 2 * i + u
                    dve.wait_ge(stored[u], 16 * i + 16)
                    for s in range(SUB):
                        dve.wait_ge(xb_done, 4 * g + s + 1)
                        dve.wait_ge(yp_done, 4 * g + s + 1)
                        nc.vector.tensor_tensor(y[:, u, s, :], yp[:, s % 2, 0:D], xb[:, u, s, :], ALU.add).then_inc(y_done, 1)

        @block.scalar
        def _(act):
            with act.Fori(0, NG) as g:
                for s in range(SUB):
                    act.wait_ge(tr_done, 4 * g + s + 1)
                    nc.scalar.activation(oT[:, s % 2, :, :], tr[:, s % 2, 0:D].rearrange("p (c n) -> p c n", c=DC),
                                         ACT.Copy).then_inc(oT_done, 1)

        @block.tensor
        def _(pe):
            pe.sem_inc(oT_done, 2)
            pe.wait_ge(weights, 32)

            def turn_tile(g, u, s):
                pe.wait_ge(oT_done, 4 * g + s + 1)
                for c in range(DC):
                    last = nc.tensor.transpose(tr[:, s % 2, P * c:P * c + P], o[:, u, s, P * c:P * c + P], ident[:, :])
                last.then_inc(tr_done, 1)

            with pe.Fori(0, NG // 2) as i:
                for u in range(2):
                    g = 2 * i + u
                    pe.wait_ge(loaded[u], 32 * i + 32)
                    turn_tile(g, u, 0)
                    for s in range(SUB):
                        if s + 1 < SUB:
                            turn_tile(g, u, s + 1)
                        pe.wait_ge(oT_done, 4 * g + s + 3)
                        pe.wait_ge(y_done, 4 * g + s + 3)
                        for c in range(DC):
                            last = nc.tensor.matmul(yp[:, s % 2, 0:D], oT[:, s % 2, c, :], wo[:, c, :],
                                                    start=c == 0, stop=c == DC - 1)
                        last.then_inc(yp_done, 1)


H2 = 8
HD2 = 64
INNER = H2 * HD2
HALF = HD2 // 2
KC = INNER // P
SCALE2 = 8.0


def shifted(t):
    a = t[1:N + 1, 0:D // 2].rearrange("(t p) d -> t p d", p=P)
    b = t[0:N, D // 2:D].rearrange("(t p) d -> t p d", p=P)
    return a, b


def window_attention(nc, layer, w_qkv, scales_d, w_o, tables_d, ident, identb, x_d, mid_d):
    with Frame(nc, f"win{layer}") as f:
        wqkv = f.sb("wqkv", [P, DC, 3 * INNER])
        wo = f.sb("wo", [P, KC, D])
        scales = f.sb("scales", [P, 4 * HD2])
        mask = f.sb("mask", [P, 2, 2, 2 * P], BF16)
        half = f.sb("half", [P, 2 * H2])
        h = f.sb("h", [P, 2, D])
        x = f.sb("x", [P, 2, D])
        tab = f.sb("tab", [P, 2, 4 * HD2])
        tq = f.sb("tq", [P, 2, 2, 2, HD2])
        hT = f.sb("hT", [P, DC, P])
        square = f.sb("square", [P, 2 * INNER])
        ss = f.sb("ss", [P, 2 * H2])
        ssm = f.sb("ssm", [P, 2 * H2])
        rn = f.sb("rn", [P, 2 * H2])
        direct = f.sb("direct", [P, 2, H2, HD2])
        crossed = f.sb("crossed", [P, 2, H2, HD2])
        turned = f.sb("turned", [P, 2, H2, HD2])
        unit = f.sb("unit", [P, 2, 2, H2, HD2])
        qT = f.sb("qT", [P, KC, P])
        kT = f.sb("kT", [P, 2, KC, P])
        v = f.sb("v", [P, 2, H2, HD2])
        peak = f.sb("peak", [P, H2])
        bias = f.sb("bias", [P, H2])
        prob = f.sb("prob", [P, H2, 2 * P])
        total = f.sb("total", [P, H2])
        rec = f.sb("rec", [P, H2])
        probT = f.sb("probT", [P, 4, 4, P])
        o = f.sb("o", [P, H2, HD2])
        oT = f.sb("oT", [P, KC, P])
        y = f.sb("y", [P, 2, D])
        tp = f.psum("tp", [P, 512])
        qkv = f.psum("qkv", [P, 3, 512])
        sc = f.psum("sc", [P, 4, 512])

        weights = f.sem("weights")
        cleared = f.sem("cleared")
        cleared_v = f.sem("cleared_v")
        mask_made = f.sem("mask_made")
        loaded = [f.sem(f"loaded{w}") for w in range(2)]
        x_loaded = [f.sem(f"x_loaded{w}") for w in range(2)]
        tp_done = f.sem("tp_done")
        hT_done = f.sem("hT_done")
        qkv_done = f.sem("qkv_done")
        square_done = f.sem("square_done")
        ss_done = f.sem("ss_done")
        ssm_done = f.sem("ssm_done")
        rn_done = f.sem("rn_done")
        tq_done = f.sem("tq_done")
        products = f.sem("products")
        turned_done = f.sem("turned_done")
        unit_done = f.sem("unit_done")
        up_done = f.sem("up_done")
        qT_done = f.sem("qT_done")
        kT_done = f.sem("kT_done")
        s_done = f.sem("s_done")
        peak_done = f.sem("peak_done")
        bias_done = f.sem("bias_done")
        p_done = f.sem("p_done")
        pt_done = f.sem("pt_done")
        probT_done = f.sem("probT_done")
        pv_done = f.sem("pv_done")
        v_done = f.sem("v_done")
        rec_done = f.sem("rec_done")
        o_done = f.sem("o_done")
        ot_done = f.sem("ot_done")
        oT_done = f.sem("oT_done")
        yp_done = f.sem("yp_done")
        y_done = f.sem("y_done")
        turn = f.sem("turn")
        stored = [f.sem(f"stored{w}") for w in range(2)]
        block = f.block()
        ha, hb = shifted(x_d)
        xt = x_d[1:N + 1, :].rearrange("(t p) d -> t p d", p=P)
        mt = mid_d[1:N + 1, :].rearrange("(t p) d -> t p d", p=P)
        tabt = tables_d.rearrange("(t p) d -> t p d", p=P)
        LOADS = 48

        @block.sync
        def _(sp):
            def load(t, w):
                sp.dma_start(h[:, w, 0:D // 2], ha[t]).then_inc(loaded[w], 16)
                sp.dma_start(h[:, w, D // 2:D], hb[t]).then_inc(loaded[w], 16)
                sp.dma_start(tab[:, w, :], tabt[t]).then_inc(loaded[w], 16)

            for w in range(2):
                sp.sem_inc(stored[w], 16)
            load(0, 0)
            sp.dma_start(wqkv[:, :, :], rows(w_qkv)).then_inc(weights, 16)
            sp.dma_start(wo[:, :, :], rows(w_o)).then_inc(weights, 16)
            sp.dma_start(scales[:, :], spread(scales_d)).then_inc(weights, 16)
            load(1, 1)
            for w in range(2):
                sp.dma_start(x[:, w, :], xt[w]).then_inc(x_loaded[w], 16)
            with sp.Fori(0, NT // 2) as i:
                for w in range(2):
                    t = 2 * i + w
                    sp.wait_ge(tp_done, t + 1)
                    sp.wait_ge(tq_done, t + 1)
                    sp.sem_inc(turn, 1)
                    load((t + 2) % NT, w)
                    sp.wait_ge(y_done, t + 1)
                    sp.dma_start(mt[t], y[:, w, :]).then_inc(stored[w], 16)
                    sp.dma_start(x[:, w, :], xt[(t + 2) % NT]).then_inc(x_loaded[w], 16)
            for w in range(2):
                sp.wait_ge(loaded[w], LOADS * (NT // 2 + 1))
                sp.wait_ge(x_loaded[w], 16 * (NT // 2 + 1))
                sp.wait_ge(stored[w], 16 * (NT // 2) + 16)

        @block.gpsimd
        def _(pool):
            nc.gpsimd.memset(mask[:, :, :, :], 0.0).then_inc(mask_made, 1)
            nc.gpsimd.memset(half[:, :], -0.5).then_inc(cleared, 1)
            pool.wait_ge(mask_made, 1)
            nc.gpsimd.memset(mask[:, 0, :, 0:P], -1e30).then_inc(mask_made, 1)
            nc.gpsimd.affine_select(out=mask[:, 1, :, 0:P], in_=mask[:, 1, :, 0:P], compare_op=ALU.is_ge, fill=-1e30,
                                    base=0, pattern=[[0, 2], [1, P]], channel_multiplier=-1).then_inc(mask_made, 1)
            for first in range(2):
                nc.gpsimd.affine_select(out=mask[:, first, :, P:2 * P], in_=mask[:, first, :, P:2 * P], compare_op=ALU.is_ge,
                                        fill=-1e30, base=0, pattern=[[0, 2], [-1, P]], channel_multiplier=1).then_inc(mask_made, 1)
            pool.wait_ge(cleared, 1)
            pool.wait_ge(weights, 48)

            def prepare(g, w, i):
                pool.wait_ge(loaded[w], LOADS * i + LOADS)
                nc.gpsimd.tensor_tensor(tq[:, w, :, :, :].rearrange("p q c d -> p (q c d)"), tab[:, w, :], scales[:, :],
                                        ALU.mult).then_inc(tq_done, 1)
                pool.wait_ge(ssm_done, g + 1)
                nc.gpsimd.tensor_tensor(rn[:, :], ssm[:, :], half[:, :], ALU.pow).then_inc(rn_done, 1)

            prepare(0, 0, 0)
            with pool.Fori(0, NT // 2) as i:
                for w in range(2):
                    prepare(2 * i + w + 1, 1 - w, i + w)

        @block.vector
        def _(dve):
            nc.vector.memset(v[:, 1, :, :], 0.0).then_inc(cleared_v, 1)
            nc.vector.memset(kT[:, 1, :, :], 0.0).then_inc(cleared_v, 1)

            def multiply(g, w):
                dve.wait_ge(square_done, g + 1)
                nc.vector.tensor_reduce(ss[:, :], square[:, :].rearrange("p (h d) -> p h d", d=HD2), AX.X, ALU.add).then_inc(ss_done, 1)
                dve.wait_ge(ss_done, g + 1)
                nc.vector.tensor_scalar(ssm[:, :], ss[:, :], 1e-24, None, ALU.max).then_inc(ssm_done, 1)
                dve.wait_ge(tq_done, g + 1)
                x4 = qkv[:, 0:2, :].rearrange("p q (h d) -> p q h d", d=HD2)
                for q in range(2):
                    for out, a, b, c in ((direct, slice(0, HD2), slice(0, HD2), 0), (crossed, slice(0, HALF), slice(HALF, HD2), 1),
                                         (crossed, slice(HALF, HD2), slice(0, HALF), 1)):
                        n = a.stop - a.start
                        last = nc.vector.tensor_tensor(out[:, q, :, a], x4[:, q, :, b],
                                                       tq[:, w, q, c:c + 1, a].broadcast_to([P, H2, n]), ALU.mult)
                last.then_inc(products, 1)

            def rotate(g, w):
                dve.wait_ge(products, g + 1)
                nc.vector.tensor_tensor(turned[:, :, :, :].rearrange("p q h d -> p (q h d)"),
                                        direct[:, :, :, :].rearrange("p q h d -> p (q h d)"),
                                        crossed[:, :, :, :].rearrange("p q h d -> p (q h d)"), ALU.add).then_inc(turned_done, 1)
                dve.wait_ge(turned_done, g + 1)
                dve.wait_ge(rn_done, g + 1)
                nc.vector.tensor_tensor(unit[:, w, :, :, :].rearrange("p q h d -> p (q h) d"),
                                        turned[:, :, :, :].rearrange("p q h d -> p (q h) d"),
                                        rn[:, :].unsqueeze(2).broadcast_to([P, 2 * H2, HD2]), ALU.mult).then_inc(unit_done, 1)

            def add(t, w, i):
                dve.wait_ge(yp_done, t + 1)
                dve.wait_ge(x_loaded[w], 16 * i + 16)
                dve.wait_ge(stored[w], 16 * i + 16)
                nc.vector.tensor_tensor(y[:, w, :], tp[:, 0:D], x[:, w, :], ALU.add).then_inc(y_done, 1)

            def step(t, w, i, first):
                dve.wait_ge(s_done, t + 1)
                nc.vector.tensor_reduce(peak[:, :], sc[:, :, :].rearrange("p b (j k) -> p (b j) k", j=2), AX.X, ALU.max).then_inc(peak_done, 1)
                dve.wait_ge(peak_done, t + 1)
                nc.vector.tensor_scalar(bias[:, :], peak[:, :], -SCALE2, None, ALU.mult).then_inc(bias_done, 1)
                multiply(t + 1, 1 - w)
                if not first:
                    add(t - 1, 1 - w, i + w - 1)
                rotate(t + 1, 1 - w)
                dve.wait_ge(p_done, H2 * t + H2)
                nc.vector.reciprocal(rec[:, :], total[:, :]).then_inc(rec_done, 1)
                dve.wait_ge(pv_done, t + 1)
                dve.wait_ge(rec_done, t + 1)
                nc.vector.tensor_tensor(o[:, :, :], sc[:, 0, :].rearrange("p (h d) -> p h d", d=HD2),
                                        rec[:, :].unsqueeze(2).broadcast_to([P, H2, HD2]), ALU.mult).then_inc(o_done, 1)

            multiply(0, 0)
            rotate(0, 0)
            step(0, 0, 0, True)
            step(1, 1, 0, False)
            with dve.Fori(1, NT // 2) as i:
                for w in range(2):
                    step(2 * i + w, w, i, False)
            add(NT - 1, 1, NT // 2 - 1)

        @block.scalar
        def _(act):
            def take(g):
                act.wait_ge(tp_done, g + 1)
                nc.scalar.activation(hT[:, :, :], tp[:, 0:D].rearrange("p (c n) -> p c n", c=DC), ACT.Copy).then_inc(hT_done, 1)

            def raise_squares(g):
                act.wait_ge(qkv_done, g + 1)
                nc.scalar.activation(square[:, :], qkv[:, 0:2, :].rearrange("p b n -> p (b n)"), ACT.Square).then_inc(square_done, 1)

            def take_v(g, w):
                nc.scalar.activation(v[:, w, :, :], qkv[:, 2, :].rearrange("p (h d) -> p h d", d=HD2), ACT.Copy).then_inc(v_done, 1)

            def take_o(t):
                act.wait_ge(ot_done, t + 1)
                nc.scalar.activation(oT[:, :, :], tp[:, :].rearrange("p (a n) -> p a n", a=KC), ACT.Copy).then_inc(oT_done, 1)

            def step(t, w, first):
                act.wait_ge(up_done, 2 * t + 1)
                nc.scalar.activation(qT[:, :, :], sc[:, 2, :].rearrange("p (a n) -> p a n", a=KC), ACT.Copy).then_inc(qT_done, 1)
                act.wait_ge(up_done, 2 * t + 2)
                nc.scalar.activation(kT[:, w, :, :], sc[:, 3, :].rearrange("p (a n) -> p a n", a=KC), ACT.Copy).then_inc(kT_done, 1)
                take(t + 1)
                if not first:
                    take_o(t - 1)
                for b in range(4):
                    for j in range(2):
                        if b == j == 0:
                            act.wait_ge(bias_done, t + 1)
                        k = 2 * b + j
                        head = 2 * (b // 2 * 2 + j) + b % 2
                        nc.scalar.activation(prob[:, k, :], sc[:, b, 2 * P * j:2 * P * j + 2 * P], ACT.Exp, bias=bias[:, k:k + 1],
                                             scale=SCALE2, accum_out=total[:, head:head + 1]).then_inc(p_done, 1)
                raise_squares(t + 1)
                for b in range(4):
                    act.wait_ge(pt_done, 4 * t + b + 1)
                    nc.scalar.activation(probT[:, b, :, :], sc[:, b, :].rearrange("p (a n) -> p a n", a=4), ACT.Copy).then_inc(probT_done, 1)
                act.wait_ge(pv_done, t + 1)
                take_v(t + 1, 1 - w)

            take(0)
            raise_squares(0)
            take_v(0, 0)
            step(0, 0, True)
            step(1, 1, False)
            with act.Fori(1, NT // 2) as i:
                for w in range(2):
                    step(2 * i + w, w, False)
            take_o(NT - 1)

        @block.tensor
        def _(pe):
            pe.wait_ge(weights, 48)
            pe.wait_ge(cleared_v, 2)
            pe.wait_ge(mask_made, 5)

            def turn_tile(g, w, i, first):
                pe.wait_ge(loaded[w], LOADS * i + LOADS)
                if not first:
                    pe.wait_ge(y_done, g - 2)
                for c in range(DC):
                    last = nc.tensor.transpose(tp[:, P * c:P * c + P], h[:, w, P * c:P * c + P], ident[:, :])
                last.then_inc(tp_done, 1)

            def project(g, first):
                pe.wait_ge(hT_done, g + 1)
                if not first:
                    pe.wait_ge(unit_done, g)
                    pe.wait_ge(v_done, g)
                for b in range(3):
                    for c in range(DC):
                        last = nc.tensor.matmul(qkv[:, b, :], hT[:, c, :], wqkv[:, c, INNER * b:INNER * b + INNER],
                                                start=c == 0, stop=c == DC - 1)
                last.then_inc(qkv_done, 1)

            def turn_outputs(t):
                for a in range(KC):
                    last = nc.tensor.transpose(tp[:, P * a:P * a + P], o[:, 2 * a:2 * a + 2, :].rearrange("p h d -> p (h d)"), ident[:, :])
                last.then_inc(ot_done, 1)

            def project_outputs(t):
                pe.wait_ge(oT_done, t + 1)
                for a in range(KC):
                    last = nc.tensor.matmul(tp[:, 0:D], oT[:, a, :], wo[:, a, :], start=a == 0, stop=a == KC - 1)
                last.then_inc(yp_done, 1)

            def hide(b, first):
                nc.tensor.matmul(sc[:, b, :], identb[:, :], mask[:, 0 if first else 1, :, :].rearrange("p j k -> p (j k)"),
                                 start=True, stop=False)

            def step(t, w, i, first, second):
                pe.wait_ge(unit_done, t + 1)
                for q in range(2):
                    for a in range(KC):
                        last = nc.tensor.transpose(sc[:, 2 + q, P * a:P * a + P],
                                                   unit[:, w, q, 2 * a:2 * a + 2, :].rearrange("p h d -> p (h d)"), ident[:, :])
                    last.then_inc(up_done, 1)
                turn_tile(t + 1, 1 - w, i + w, first or second)
                if not first:
                    pe.wait_ge(o_done, t)
                hide(0, first)
                hide(1, first)
                pe.wait_ge(qT_done, t + 1)
                pe.wait_ge(kT_done, t + 1)
                hide(2, first)
                hide(3, first)
                for b in range(4):
                    e = b % 2
                    for j in range(2):
                        a = b // 2 * 2 + j
                        side = slice(HD2 * e, HD2 * e + HD2)
                        for k, tile in enumerate((1 - w, w)):
                            last = nc.tensor.matmul(sc[:, b, 2 * P * j + P * k:2 * P * j + P * k + P], qT[side, a, :],
                                                    kT[side, tile, a, :], start=False, stop=j == k == 1)
                last.then_inc(s_done, 1)
                if not first:
                    pe.wait_ge(hT_done, t + 2)
                    turn_outputs(t - 1)
                project(t + 1, False)
                if not first:
                    project_outputs(t - 1)
                for b in range(4):
                    pe.wait_ge(p_done, H2 * t + 2 * b + 2)
                    for j in range(2):
                        for k in range(2):
                            last = nc.tensor.transpose(sc[:, b, P * (2 * j + k):P * (2 * j + k) + P],
                                                       prob[:, 2 * b + j, P * k:P * k + P], ident[:, :])
                    last.then_inc(pt_done, 1)
                for b in range(4):
                    pe.wait_ge(probT_done, 4 * t + b + 1)
                    for j in range(2):
                        head = 2 * (b // 2 * 2 + j) + b % 2
                        for k, tile in enumerate((1 - w, w)):
                            last = nc.tensor.matmul(sc[:, 0, HD2 * head:HD2 * head + HD2], probT[:, b, 2 * j + k, :],
                                                    v[:, tile, head, :], start=k == 0, stop=k == 1, skip_group_check=True)
                last.then_inc(pv_done, 1)

            turn_tile(0, 0, 0, True)
            project(0, True)
            step(0, 0, 0, True, False)
            step(1, 1, 0, False, True)
            with pe.Fori(1, NT // 2) as i:
                for w in range(2):
                    step(2 * i + w, w, i, False, False)
            pe.wait_ge(y_done, NT - 1)
            pe.wait_ge(o_done, NT)
            turn_outputs(NT - 1)
            project_outputs(NT - 1)


HID = int(D * 4 * 2 / 3)
HC = -(-HID // P)
LAST = HID - P * (HC - 1)


def feed_forward_1(nc, layer, w_1, b1c_d, w_2, b_2, ln_g, ln_b, ident, mid_d, extra, out_d):
    with Frame(nc, f"ff{layer}") as f:
        w1 = f.sb("w1", [P, DC, 2 * HID])
        w2 = f.sb("w2", [P, HC, D])
        b1c = f.sb("b1c", [P, 2 * HC])
        b2r = f.sb("b2r", [P, D])
        gm = f.sb("gm", [P, D])
        bt = f.sb("bt", [P, D])
        half = f.sb("half", [P, SUB])
        eps = f.sb("eps", [P, SUB])
        h = f.sb("h", [P, 2, SUB, D])
        x = f.sb("x", [P, 2, SUB, D])
        more = f.sb("more", [P, 2, SUB, D])
        stats = f.sb("stats", [P, SUB, 6])
        mv = f.sb("mv", [P, SUB, 2])
        ve = f.sb("ve", [P, SUB])
        rstd = f.sb("rstd", [P, SUB])
        z = f.sb("z", [P, 2, SUB, D])
        zg = f.sb("zg", [P, 2, SUB, D])
        zb = f.sb("zb", [P, 2, SUB, D])
        zT = f.sb("zT", [P, DC, GROUP])
        gate = f.sb("gate", [P, 2, GROUP])
        hid = f.sb("hid", [P, HC, GROUP])
        xb = f.sb("xb", [P, 2, SUB, D])
        y = f.sb("y", [P, 2, SUB, D])
        tr = f.psum("tr", [P, 2, 512])
        up = f.psum("up", [P, 2, 512])
        gp = f.psum("gp", [P, 2, 512])
        op = f.psum("op", [P, 2, 512])

        weights = f.sem("weights")
        prepared = f.sem("prepared")
        loaded = [f.sem(f"loaded{u}") for u in range(2)]
        stats_done = f.sem("stats_done")
        pace = f.sem("pace")
        var_done = f.sem("var_done")
        var_eps = f.sem("var_eps")
        rstd_done = f.sem("rstd_done")
        z_done = f.sem("z_done")
        zg_done = f.sem("zg_done")
        zb_done = f.sem("zb_done")
        xb_first = f.sem("xb_first")
        xb_done = f.sem("xb_done")
        tr_done = f.sem("tr_done")
        zT_done = f.sem("zT_done")
        gp_done = f.sem("gp_done")
        up_done = f.sem("up_done")
        gate_done = f.sem("gate_done")
        hid_done = f.sem("hid_done")
        op_done = f.sem("op_done")
        y_done = f.sem("y_done")
        turn = f.sem("turn")
        stored = [f.sem(f"stored{u}") for u in range(2)]
        block = f.block()
        ha = mid_d[1:N + 1, 0:D // 2].rearrange("(g s p) d -> g p s d", s=SUB, p=P)
        hb = mid_d[0:N, D // 2:D].rearrange("(g s p) d -> g p s d", s=SUB, p=P)
        xg = tiles(mid_d[1:N + 1, :])
        LOADS = 64 if extra is not None else 48

        @block.sync
        def _(sp):
            def load(g, u):
                sp.dma_start(h[:, u, :, 0:D // 2], ha[g]).then_inc(loaded[u], 16)
                sp.dma_start(h[:, u, :, D // 2:D], hb[g]).then_inc(loaded[u], 16)
                sp.dma_start(x[:, u, :, :], xg[g]).then_inc(loaded[u], 16)
                if extra is not None:
                    sp.dma_start(more[:, u, :, :], tiles(extra)[g]).then_inc(loaded[u], 16)

            for u in range(2):
                sp.sem_inc(stored[u], 16)
            load(0, 0)
            sp.dma_start(gm[:, :], spread(ln_g)).then_inc(weights, 16)
            sp.dma_start(bt[:, :], spread(ln_b)).then_inc(weights, 16)
            sp.dma_start(b2r[:, :], spread(b_2)).then_inc(weights, 16)
            sp.dma_start(b1c[:, :], b1c_d).then_inc(weights, 16)
            sp.dma_start(w1[:, :, :], rows(w_1)).then_inc(weights, 16)
            sp.dma_start(w2[:, 0:HC - 1, :], rows(w_2[0:P * (HC - 1), :])).then_inc(weights, 16)
            sp.dma_start(w2[0:LAST, HC - 1, :], w_2[P * (HC - 1):HID, :]).then_inc(weights, 16)
            load(1, 1)
            with sp.Fori(0, NG // 2) as i:
                for u in range(2):
                    g = 2 * i + u
                    sp.wait_ge(xb_done, 4 * g + 4)
                    sp.sem_inc(turn, 1)
                    load((g + 2) % NG, u)
                    sp.wait_ge(y_done, 4 * g + 4)
                    sp.dma_start(tiles(out_d)[g], y[:, u, :, :]).then_inc(stored[u], 16)
            for u in range(2):
                sp.wait_ge(loaded[u], LOADS * (NG // 2 + 1))
                sp.wait_ge(stored[u], 16 + 16 * (NG // 2))

        @block.gpsimd
        def _(pool):
            nc.gpsimd.memset(half[:, :], -0.5).then_inc(prepared, 1)
            nc.gpsimd.memset(eps[:, :], EPS).then_inc(prepared, 1)
            pool.wait_ge(prepared, 2)
            pool.wait_ge(weights, 112)

            def norm(g, u, i):
                pool.wait_ge(loaded[u], LOADS * i + LOADS)
                pool.wait_ge(var_done, 4 * g + 4)
                nc.gpsimd.tensor_tensor(ve[:, :], mv[:, :, 1], eps[:, :], ALU.add).then_inc(var_eps, 1)
                pool.wait_ge(var_eps, g + 1)
                nc.gpsimd.tensor_tensor(rstd[:, :], ve[:, :], half[:, :], ALU.pow).then_inc(rstd_done, 1)
                for s in range(SUB):
                    pool.wait_ge(z_done, 4 * g + s + 1)
                    nc.gpsimd.tensor_tensor(zg[:, u, s, :], z[:, u, s, :], gm[:, :], ALU.mult).then_inc(zg_done, 1)
                for s in range(SUB):
                    pool.wait_ge(zg_done, 4 * g + s + 1)
                    nc.gpsimd.tensor_tensor(zb[:, u, s, :], zg[:, u, s, :], bt[:, :], ALU.add).then_inc(zb_done, 1)
                for s in range(SUB):
                    last = nc.gpsimd.tensor_tensor(xb[:, u, s, :], x[:, u, s, :], b2r[:, :], ALU.add)
                    last.then_inc(xb_done if extra is None else xb_first, 1)
                if extra is not None:
                    for s in range(SUB):
                        pool.wait_ge(xb_first, 4 * g + s + 1)
                        nc.gpsimd.tensor_tensor(xb[:, u, s, :], xb[:, u, s, :], more[:, u, s, :], ALU.add).then_inc(xb_done, 1)

            norm(0, 0, 0)
            with pool.Fori(0, NG // 2) as i:
                for u in range(2):
                    norm(2 * i + u + 1, 1 - u, i + u)

        @block.vector
        def _(dve):
            def norm(g, u, i):
                dve.wait_ge(loaded[u], LOADS * i + LOADS)
                for s in range(SUB):
                    nc.vector.bn_stats(stats[:, s, :], h[:, u, s, :]).then_inc(stats_done, 1)
                dve.wait_ge(stats_done, 4 * g + 4)
                dve.sem_inc(pace, 1)
                for s in range(SUB):
                    nc.vector.bn_aggr(mv[:, s, :], stats[:, s, :]).then_inc(var_done, 1)
                dve.wait_ge(var_done, 4 * g + 4)
                dve.wait_ge(rstd_done, g + 1)
                for s in range(SUB):
                    nc.vector.tensor_scalar(z[:, u, s, :], h[:, u, s, :], mv[:, s, 0:1], rstd[:, s:s + 1],
                                            ALU.subtract, ALU.mult).then_inc(z_done, 1)

            dve.sem_inc(hid_done, 2)
            norm(0, 0, 0)
            with dve.Fori(0, NG // 2) as i:
                for u in range(2):
                    g = 2 * i + u
                    norm(g + 1, 1 - u, i + u)
                    for c in range(HC):
                        r = P if c < HC - 1 else LAST
                        dve.wait_ge(up_done, HC * g + c + 1)
                        dve.wait_ge(gate_done, HC * g + c + 1)
                        nc.vector.scalar_tensor_tensor(hid[0:r, c, :], up[0:r, c % 2, :], b1c[0:r, c:c + 1], gate[0:r, c % 2, :],
                                                       ALU.add, ALU.mult).then_inc(hid_done, 1)
                    dve.wait_ge(stored[u], 16 * i + 16)
                    for s in range(SUB):
                        dve.wait_ge(op_done, 4 * g + s + 1)
                        dve.wait_ge(xb_done, 4 * g + s + 1)
                        nc.vector.tensor_tensor(y[:, u, s, :], op[:, s % 2, 0:D], xb[:, u, s, :], ALU.add).then_inc(y_done, 1)

        @block.scalar
        def _(act):
            act.wait_ge(weights, 112)
            with act.Fori(0, NG // 2) as i:
                for u in range(2):
                    g = 2 * i + u
                    for s in range(SUB):
                        act.wait_ge(tr_done, 4 * g + s + 1)
                        nc.scalar.activation(zT[:, :, P * s:P * s + P], tr[:, s % 2, 0:D].rearrange("p (c n) -> p c n", c=DC),
                                             ACT.Copy).then_inc(zT_done, 1)
                    for c in range(HC):
                        r = P if c < HC - 1 else LAST
                        act.wait_ge(gp_done, HC * g + c + 1)
                        act.wait_ge(hid_done, HC * g + c + 1)
                        nc.scalar.activation(gate[0:r, c % 2, :], gp[0:r, c % 2, :], ACT.Gelu, bias=b1c[0:r, HC + c:HC + c + 1]).then_inc(gate_done, 1)

        @block.tensor
        def _(pe):
            pe.wait_ge(weights, 112)

            def forward(g, u, first):
                for s in range(SUB):
                    pe.wait_ge(zb_done, 4 * g + s + 1)
                    if s >= 2:
                        pe.wait_ge(zT_done, 4 * g + s - 1)
                    for c in range(DC):
                        last = nc.tensor.transpose(tr[:, s % 2, P * c:P * c + P], zb[:, u, s, P * c:P * c + P], ident[:, :])
                    last.then_inc(tr_done, 1)
                pe.wait_ge(zT_done, 4 * g + 4)
                for m in range(HC):
                    r = P if m < HC - 1 else LAST
                    if m >= 2:
                        pe.wait_ge(gate_done, HC * g + m - 1)
                    for c in range(DC):
                        last = nc.tensor.matmul(gp[0:r, m % 2, :], w1[:, c, HID + P * m:HID + P * m + r], zT[:, c, :],
                                                start=c == 0, stop=c == DC - 1)
                    last.then_inc(gp_done, 1)
                    pe.wait_ge(hid_done, HC * g + m + 1)
                    for c in range(DC):
                        last = nc.tensor.matmul(up[0:r, m % 2, :], w1[:, c, P * m:P * m + r], zT[:, c, :],
                                                start=c == 0, stop=c == DC - 1)
                    last.then_inc(up_done, 1)
                pe.wait_ge(hid_done, HC * g + HC + 2)
                for s in range(SUB):
                    if s >= 2 or not first:
                        pe.wait_ge(y_done, 4 * g + s - 1)
                    for c in range(HC):
                        r = P if c < HC - 1 else LAST
                        last = nc.tensor.matmul(op[:, s % 2, 0:D], hid[0:r, c, P * s:P * s + P], w2[0:r, c, :],
                                                start=c == 0, stop=c == HC - 1)
                    last.then_inc(op_done, 1)

            forward(0, 0, True)
            forward(1, 1, False)
            with pe.Fori(1, NG // 2) as i:
                for u in range(2):
                    forward(2 * i + u, u, False)


def clear_rows(nc, targets):
    with Frame(nc, "edge") as f:
        zero = f.sb("zero", [1, D])
        cleared = f.sem("cleared")
        stored = f.sem("stored")
        block = f.block()

        @block.vector
        def _(dve):
            nc.vector.memset(zero[:, :], 0.0).then_inc(cleared, 1)

        @block.sync
        def _(sp):
            sp.wait_ge(cleared, 1)
            for t in targets:
                sp.dma_start(t[0:1, :], zero[:, :]).then_inc(stored, 16)
            sp.wait_ge(stored, 16 * len(targets))


def setup(nc, proj, projbd):
    with Frame(nc, "setup") as f:
        cleared = f.sem("cleared")
        placed = f.sem("placed")
        block = f.block()

        @block.vector
        def _(dve):
            nc.vector.memset(projbd[:, :, :], 0.0).then_inc(cleared, 1)

        @block.sync
        def _(sp):
            sp.wait_ge(cleared, 1)
            for h in range(H0):
                k = h % PAIRS
                sp.dma_start(projbd[HD0 * k:HD0 * k + HD0, h // PAIRS, F0 * k:F0 * k + F0], proj[h]).then_inc(placed, 16)
            sp.wait_ge(placed, 16 * H0)


DEPTH1 = 2
WINDOW = P


def program(nc, a, out):
    def dram(name, shape, dt=F32):
        return nc.dram_tensor(name, shape, dt, kind="Internal").ap()

    xn_d = dram("xn_d", (N, D))
    xnT_d = dram("xnT_d", (D, N))
    y_d = dram("y_d", (N, D))
    res_d = dram("res_d", (N, D))
    x1_d = dram("x1_d", (N, D))
    xn1_d = dram("xn1_d", (N + 1, D))
    lay_d = dram("lay_d", (N + 1, D))
    mid_d = [dram(f"mid{l}_d", (N + 1, D)) for l in range(DEPTH1)]
    qk_d = dram("qk_d", (2, PARTS, D, N), BF16)
    v_d = dram("v_d", (NG, P, H1, SUB, VC), BF16)
    o_d = dram("o_d", (N, D))
    sum_d = dram("sum_d", (N, D))
    x = a["L0_attn_x"].rearrange("a n d -> (a n) d")
    with Frame(nc, "keep") as keep:
        ident = keep.sb("ident", [P, P])
        identb = keep.sb("identb", [P, P], BF16)
        causal_q = keep.sb("causal_q", [P, P], BF16)
        causal_k = keep.sb("causal_k", [P, P], BF16)
        constants(nc, ident, identb, causal_q, causal_k)
        clear_rows(nc, [xn1_d, lay_d, *mid_d])
        with Frame(nc, "layer0") as f:
            projbd = f.sb("projbd", [P, DC, GROUP])
            kvbd = f.sb("kvbd", [P, PAIRS, 2 * VW])
            setup(nc, a["L0_attn_proj"], projbd)
            linear_attention_keys(nc, x, a["w_qkvT"], projbd, kvbd, ident, xn_d, xnT_d)
            linear_attention_queries(nc, a["w_qkvT"], a["w_outT"], a["L0_attn_b_out"], a["L0_attn_gamma"],
                                     a["L0_attn_beta"], projbd, kvbd, ident, xn_d, xnT_d, y_d)
        experts(nc, x, a["router_wT"], a["L0_ffn_router_b"], a["expert_wT"], a["L0_ffn_expert_b"], ident, xnT_d, res_d)
        feed_forward_0(nc, a["w1T"], a["b1_columns"], a["w2T"], a["L0_attn_b2"], a["L0_attn_gamma"], a["L0_attn_beta"],
                       ident, y_d, res_d, x1_d, xn1_d)
        latent_projections(nc, a, a["rope_cos"], a["rope_sin"], ident, xn1_d, qk_d, v_d)
        latent_attention(nc, a["part_sum"], ident, identb, causal_q, causal_k, qk_d, v_d, o_d)
        latent_output(nc, a["L1_attn_wo"], a["L1_attn_bo"], ident, o_d, x1_d, sum_d)
        source = xn1_d
        for l in range(DEPTH1):
            end = l == DEPTH1 - 1
            window_attention(nc, l, a["L1_ffn_wqkv"][l], a["scales"][l], a["L1_ffn_wo"][l], a["tables"], ident, identb,
                             source, mid_d[l])
            feed_forward_1(nc, l, a["L1_ffn_w1"][l], a["b1_halves"][l], a["L1_ffn_w2"][l], a["L1_ffn_b2"][l],
                           a["L1_ffn_ln_g"][l], a["L1_ffn_ln_b"][l], ident, mid_d[l], sum_d if end else None,
                           out.rearrange("a n d -> (a n) d") if end else lay_d[1:N + 1, :])
            source = lay_d


def tables():
    import numpy as np

    f = np.float32
    t = np.arange(N, dtype=f)
    freq = (f(1) / f(10000) ** (np.arange(0, ROPE, 2, dtype=f) / f(ROPE))).astype(f)
    ang = (t[:, None] * freq[None, :]).astype(f)
    cos, sin = np.cos(ang), np.sin(ang)
    idx = np.arange(0, HD2, 2, dtype=f)
    freq = (f(1) / f(10000) ** (idx / f(HD2))).astype(f)
    ang = (t[:, None] * freq[None, :]).astype(f)
    base = ((idx + f(0.4 * HD2)) / f(1.4 * HD2)).astype(f)
    power = ((t - f(N // 2)) / f(WINDOW // 2)).astype(f)
    grow = (base[None, :] ** power[:, None]).astype(f)
    c, s = np.cos(ang), np.sin(ang)
    windowed = np.concatenate([c * grow, c * grow, -s * grow, s * grow, c / grow, c / grow, -s / grow, s / grow], axis=1)
    part_sum = np.zeros((VC, VW), f)
    for a in range(PARTS):
        part_sum[HD1 * a:HD1 * a + HD1, 0:HD1] = np.eye(HD1, dtype=f)
    part_sum[VC - 1, VW - 1] = 1
    return {
        "tables": np.ascontiguousarray(windowed.astype(f)),
        "part_sum": part_sum,
        "rope_cos": np.ascontiguousarray(np.concatenate([cos, cos], axis=1).T.astype(f)),
        "rope_sin": np.ascontiguousarray(np.concatenate([-sin, sin], axis=1).T.astype(f)),
    }


def kernel(**inputs):
    import numpy as _np
    import concourse.bacc as _bacc
    from concourse.bass_utils import run_bass_kernel_spmd as _run

    nc = _bacc.Bacc("TRN2", target_bir_lowering=False, num_devices=1)
    arrays = {k: _np.ascontiguousarray(v) for k, v in inputs.items()}
    arrays["w_qkvT"] = _np.ascontiguousarray(arrays.pop("L0_attn_w_qkv").T)
    arrays["w_outT"] = _np.ascontiguousarray(arrays.pop("L0_attn_w_out").T)
    arrays["w1T"] = _np.ascontiguousarray(arrays.pop("L0_attn_w1").T)
    arrays["b1_columns"] = _np.ascontiguousarray(arrays.pop("L0_attn_b1").reshape(FF0 // P, P).T)
    arrays["w2T"] = _np.ascontiguousarray(arrays.pop("L0_attn_w2").T)
    arrays["router_wT"] = _np.ascontiguousarray(arrays.pop("L0_ffn_router_w").T)
    arrays["expert_wT"] = _np.ascontiguousarray(arrays.pop("L0_ffn_expert_w").transpose(2, 0, 1))
    qs, ks = arrays.pop("L1_ffn_q_scale"), arrays.pop("L1_ffn_k_scale")
    swap = lambda v: _np.concatenate([v[:, HALF:], v[:, :HALF]], axis=1)
    arrays["scales"] = _np.ascontiguousarray(_np.concatenate([qs, swap(qs), ks, swap(ks)], axis=1))
    b1 = arrays.pop("L1_ffn_b1")
    halves = _np.zeros((DEPTH1, P, 2 * HC), b1.dtype)
    for j in range(2 * HC):
        c = j % HC
        n = min(P, HID - P * c)
        at = HID * (j // HC) + P * c
        halves[:, 0:n, j] = b1[:, at:at + n]
    arrays["b1_halves"] = halves
    arrays.update(tables())
    args = {k: nc.dram_tensor(f"in_{k}", v.shape, F32,
                              kind="ExternalInput").ap() for k, v in arrays.items()}
    out = nc.dram_tensor("out_0_dram", (1, N, D), F32, kind="ExternalOutput").ap()
    program(nc, args, out)
    r = _run(nc, [{f"in_{k}": v for k, v in arrays.items()}], core_ids=[0])
    return r.results[0]["out_0_dram"]
```
